# Optimizing a Trainium2 kernel written in Bass

```python
import numpy as np
import jax
import jax.numpy as jnp

def _softmax(x, axis=-1):
    return jax.nn.softmax(x, axis=axis)

def _gelu(x):
    return jax.nn.gelu(x, approximate=True)

def _silu(x):
    return jax.nn.silu(x)

def _sigmoid(x):
    return jax.nn.sigmoid(x)

def _layernorm(x, axis=-1, eps=1e-05):
    m = jnp.mean(x, axis=axis, keepdims=True)
    v = jnp.var(x, axis=axis, keepdims=True)
    return (x - m) / jnp.sqrt(v + eps)

def _scatter_add(tgt, idx, src, axis=0):
    return tgt.at[idx].add(src)

def _segment_sum(src, seg, n):
    return jax.ops.segment_sum(src, seg, n)
kernel_name = 'mk_vit_tower_postln_d1_tok_img256_r4_6359c8'

def setup_inputs(seed: int=0):
    np.random.seed(seed)
    _w = jnp.asarray

    def _rec_inputs():
        import jax
        import jax.numpy as jnp
        _rk = jax.random.key(seed)
        x = -0.000596345 + 1.00056 * jax.random.normal(jax.random.fold_in(_rk, 1), (64, 64, 64, 3), jnp.float32)
        return x
    x = _rec_inputs()

    def _L0_tok_setup():
        import jax, jax.numpy as jnp
        import numpy as np
        B, H, W = (16, 64, 64)
        WIDTH, LAYERS, M1, M2 = (32, 4, 12, 12)
        EPS = 1e-05

        def layer_norm(x, g, b):
            mu = jnp.mean(x, axis=-1, keepdims=True)
            var = jnp.mean((x - mu) ** 2, axis=-1, keepdims=True)
            return (x - mu) * jax.lax.rsqrt(var + EPS) * g + b

        def gelu(x):
            return jax.nn.gelu(x, approximate=False)

        def spectral_conv(x, w1, w2):
            b, c, h, w = x.shape
            x_ft = jnp.fft.rfft2(x)
            out_ft = jnp.zeros((b, w1.shape[1], h, w // 2 + 1), dtype=x_ft.dtype)
            out_ft = out_ft.at[:, :, :M1, :M2].set(jnp.einsum('bixy,ioxy->boxy', x_ft[:, :, :M1, :M2], w1))
            out_ft = out_ft.at[:, :, -M1:, :M2].set(jnp.einsum('bixy,ioxy->boxy', x_ft[:, :, -M1:, :M2], w2))
            return jnp.fft.irfft2(out_ft, s=(h, w))
        key = jax.random.key(seed)
        ks = jax.random.split(key, 16)
        scale = 1.0 / (WIDTH * WIDTH)
        d = {'x': jax.random.normal(ks[0], (B, H, W, 3), jnp.float32), 'fc0_w': jax.random.normal(ks[1], (3, WIDTH), jnp.float32) * 0.5, 'fc0_b': jnp.zeros((WIDTH,), jnp.float32), 'ln0_g': jnp.ones((WIDTH,), jnp.float32), 'ln0_b': jnp.zeros((WIDTH,), jnp.float32), 'w1r': jax.random.uniform(ks[2], (LAYERS, WIDTH, WIDTH, M1, M2), jnp.float32) * scale, 'w1i': jax.random.uniform(ks[3], (LAYERS, WIDTH, WIDTH, M1, M2), jnp.float32) * scale, 'w2r': jax.random.uniform(ks[4], (LAYERS, WIDTH, WIDTH, M1, M2), jnp.float32) * scale, 'w2i': jax.random.uniform(ks[5], (LAYERS, WIDTH, WIDTH, M1, M2), jnp.float32) * scale, 'conv_w': jax.random.normal(ks[6], (LAYERS, WIDTH, WIDTH), jnp.float32) * (1.0 / np.sqrt(WIDTH)), 'conv_b': jnp.zeros((LAYERS, WIDTH), jnp.float32), 'ln_g': jnp.ones((LAYERS, WIDTH), jnp.float32), 'ln_b': jnp.zeros((LAYERS, WIDTH), jnp.float32), 'fc1_w': jax.random.normal(ks[7], (WIDTH, 128), jnp.float32) * (1.0 / np.sqrt(WIDTH)), 'fc1_b': jnp.zeros((128,), jnp.float32), 'fc2_w': jax.random.normal(ks[8], (128, 64), jnp.float32) * (1.0 / np.sqrt(128)), 'fc2_b': jnp.zeros((64,), jnp.float32), 'fc3_w': jax.random.normal(ks[9], (64, 1), jnp.float32) * (1.0 / np.sqrt(64)), 'fc3_b': jnp.zeros((1,), jnp.float32)}
        return d
    _L0_tok_all = _L0_tok_setup()
    _L0_tok_in = {k: v for k, v in _L0_tok_all.items() if k in ('fc0_w', 'fc0_b', 'ln0_g', 'ln0_b', 'w1r', 'w1i', 'w2r', 'w2i', 'conv_w', 'conv_b', 'ln_g', 'ln_b', 'fc1_w', 'fc1_b', 'fc2_w', 'fc2_b', 'fc3_w', 'fc3_b')}
    del _L0_tok_all

    def _L0_attn_setup():
        import jax, jax.numpy as jnp
        import numpy as np
        B, L, D = (4, 1024, 64)
        key = jax.random.key(seed)
        kx, kq, kk, kv, ko = jax.random.split(key, 5)
        std = 0.02
        return {'x': jax.random.normal(kx, (B, L, D), dtype=jnp.float32), 'Wq': std * jax.random.normal(kq, (D, D), dtype=jnp.float32), 'Wk': std * jax.random.normal(kk, (D, D), dtype=jnp.float32), 'Wv': std * jax.random.normal(kv, (D, D), dtype=jnp.float32), 'Wo': std * jax.random.normal(ko, (D, D), dtype=jnp.float32)}
    _L0_attn_all = _L0_attn_setup()
    _L0_attn_in = {k: v for k, v in _L0_attn_all.items() if k in ('Wq', 'Wk', 'Wv', 'Wo')}
    del _L0_attn_all

    def _L0_ffn_setup():
        import jax, jax.numpy as jnp
        import numpy as np
        DIM = 64
        HEADS = 8
        NUM_KEYS = 64
        NUM_KV = NUM_KEYS ** 2
        PK_TOPK = 16
        FINAL_TOPK = 16
        DIM_KEY = DIM // 2
        P = 2

        def _pk(x, Wq_pk, pk_keys):
            b, n, _ = x.shape
            q = (x @ Wq_pk).reshape(b, n, P, HEADS, DIM_KEY).transpose(2, 0, 1, 3, 4)
            sim = jnp.einsum('pbnhd,pkhd->pbnhk', q, pk_keys)
            scores, idx = jax.lax.top_k(sim, PK_TOPK)
            idx0 = idx[0]
            idx1 = idx[1] * NUM_KEYS
            index = (idx0[..., :, None] + idx1[..., None, :]).reshape(b, n, HEADS, PK_TOPK * PK_TOPK)
            score = (scores[0][..., :, None] + scores[1][..., None, :]).reshape(b, n, HEADS, PK_TOPK * PK_TOPK)
            final_scores, pk_idx = jax.lax.top_k(score, FINAL_TOPK)
            final_indices = jnp.take_along_axis(index, pk_idx, axis=-1)
            final_scores = jax.nn.softmax(final_scores, axis=-1)
            return (final_scores, final_indices)
        key = jax.random.key(seed)
        ks = jax.random.split(key, 7)
        b, n = (2, 256)
        std = 0.02
        x = jax.random.normal(ks[0], (b, n, DIM), dtype=jnp.float32)
        Wq_pk = jax.random.normal(ks[1], (DIM, P * HEADS * DIM_KEY), dtype=jnp.float32) * std
        pk_keys = jax.random.normal(ks[2], (P, NUM_KEYS, HEADS, DIM_KEY), dtype=jnp.float32) * std
        Wq = jax.random.normal(ks[3], (DIM, HEADS * DIM), dtype=jnp.float32) * std
        keys_table = jax.random.normal(ks[4], (NUM_KV * HEADS, DIM), dtype=jnp.float32) * std
        values_table = jax.random.normal(ks[5], (NUM_KV * HEADS, DIM), dtype=jnp.float32) * std
        Wo = jax.random.normal(ks[6], (DIM * HEADS, DIM), dtype=jnp.float32) * std
        return {'x': x, 'Wq_pk': Wq_pk, 'pk_keys': pk_keys, 'Wq': Wq, 'keys_table': keys_table, 'values_table': values_table, 'Wo': Wo}
    _L0_ffn_all = _L0_ffn_setup()
    _L0_ffn_in = {k: v for k, v in _L0_ffn_all.items() if k in ('Wq_pk', 'pk_keys', 'Wq', 'keys_table', 'values_table', 'Wo')}
    del _L0_ffn_all
    return {'x': x, 'L0_tok_fc0_w': _L0_tok_in['fc0_w'], 'L0_tok_fc0_b': _L0_tok_in['fc0_b'], 'L0_tok_ln0_g': _L0_tok_in['ln0_g'], 'L0_tok_ln0_b': _L0_tok_in['ln0_b'], 'L0_tok_w1r': _L0_tok_in['w1r'], 'L0_tok_w1i': _L0_tok_in['w1i'], 'L0_tok_w2r': _L0_tok_in['w2r'], 'L0_tok_w2i': _L0_tok_in['w2i'], 'L0_tok_conv_w': _L0_tok_in['conv_w'], 'L0_tok_conv_b': _L0_tok_in['conv_b'], 'L0_tok_ln_g': _L0_tok_in['ln_g'], 'L0_tok_ln_b': _L0_tok_in['ln_b'], 'L0_tok_fc1_w': _L0_tok_in['fc1_w'], 'L0_tok_fc1_b': _L0_tok_in['fc1_b'], 'L0_tok_fc2_w': _L0_tok_in['fc2_w'], 'L0_tok_fc2_b': _L0_tok_in['fc2_b'], 'L0_tok_fc3_w': _L0_tok_in['fc3_w'], 'L0_tok_fc3_b': _L0_tok_in['fc3_b'], 'L0_attn_Wq': _L0_attn_in['Wq'], 'L0_attn_Wk': _L0_attn_in['Wk'], 'L0_attn_Wv': _L0_attn_in['Wv'], 'L0_attn_Wo': _L0_attn_in['Wo'], 'L0_ffn_Wq_pk': _L0_ffn_in['Wq_pk'], 'L0_ffn_pk_keys': _L0_ffn_in['pk_keys'], 'L0_ffn_Wq': _L0_ffn_in['Wq'], 'L0_ffn_keys_table': _L0_ffn_in['keys_table'], 'L0_ffn_values_table': _L0_ffn_in['values_table'], 'L0_ffn_Wo': _L0_ffn_in['Wo']}

def reference(x, L0_tok_fc0_w, L0_tok_fc0_b, L0_tok_ln0_g, L0_tok_ln0_b, L0_tok_w1r, L0_tok_w1i, L0_tok_w2r, L0_tok_w2i, L0_tok_conv_w, L0_tok_conv_b, L0_tok_ln_g, L0_tok_ln_b, L0_tok_fc1_w, L0_tok_fc1_b, L0_tok_fc2_w, L0_tok_fc2_b, L0_tok_fc3_w, L0_tok_fc3_b, L0_attn_Wq, L0_attn_Wk, L0_attn_Wv, L0_attn_Wo, L0_ffn_Wq_pk, L0_ffn_pk_keys, L0_ffn_Wq, L0_ffn_keys_table, L0_ffn_values_table, L0_ffn_Wo):
    import jax
    import jax.numpy as jnp

    def _L0_tok_ref(x, fc0_w, fc0_b, ln0_g, ln0_b, w1r, w1i, w2r, w2i, conv_w, conv_b, ln_g, ln_b, fc1_w, fc1_b, fc2_w, fc2_b, fc3_w, fc3_b):
        import jax, jax.numpy as jnp
        import numpy as np
        B, H, W = (16, 64, 64)
        WIDTH, LAYERS, M1, M2 = (32, 4, 12, 12)
        EPS = 1e-05

        def layer_norm(x, g, b):
            mu = jnp.mean(x, axis=-1, keepdims=True)
            var = jnp.mean((x - mu) ** 2, axis=-1, keepdims=True)
            return (x - mu) * jax.lax.rsqrt(var + EPS) * g + b

        def gelu(x):
            return jax.nn.gelu(x, approximate=False)

        def spectral_conv(x, w1, w2):
            b, c, h, w = x.shape
            x_ft = jnp.fft.rfft2(x)
            out_ft = jnp.zeros((b, w1.shape[1], h, w // 2 + 1), dtype=x_ft.dtype)
            out_ft = out_ft.at[:, :, :M1, :M2].set(jnp.einsum('bixy,ioxy->boxy', x_ft[:, :, :M1, :M2], w1))
            out_ft = out_ft.at[:, :, -M1:, :M2].set(jnp.einsum('bixy,ioxy->boxy', x_ft[:, :, -M1:, :M2], w2))
            return jnp.fft.irfft2(out_ft, s=(h, w))
        h = layer_norm(x @ fc0_w + fc0_b, ln0_g, ln0_b)
        h = jnp.transpose(h, (0, 3, 1, 2))
        for i in range(LAYERS):
            w1 = w1r[i] + 1j * w1i[i]
            w2 = w2r[i] + 1j * w2i[i]
            x1 = spectral_conv(h, w1, w2)
            x2 = jnp.einsum('bchw,oc->bohw', h, conv_w[i]) + conv_b[i][None, :, None, None]
            h = x1 + x2
            h = jnp.transpose(h, (0, 2, 3, 1))
            h = layer_norm(h, ln_g[i], ln_b[i])
            if i < LAYERS - 1:
                h = gelu(h)
            h = jnp.transpose(h, (0, 3, 1, 2))
        h = jnp.transpose(h, (0, 2, 3, 1))
        h = gelu(h @ fc1_w + fc1_b)
        h = gelu(h @ fc2_w + fc2_b)
        h = h @ fc3_w + fc3_b
        return h[..., 0]

    def _L0_attn_ref(x, Wq, Wk, Wv, Wo):
        import jax, jax.numpy as jnp
        import numpy as np
        B, L, D = (4, 1024, 64)
        q = x @ Wq.T
        k = x @ Wk.T
        v = x @ Wv.T
        logits = jnp.einsum('bld,bmd->blm', q, k)
        Lq = x.shape[1]
        causal_mask = jnp.triu(jnp.ones((Lq, Lq), dtype=bool), k=1)
        logits = jnp.where(causal_mask[None], jnp.asarray(0.0, logits.dtype), logits)
        attn = jax.nn.relu(logits)
        row_counts = jnp.maximum(jnp.arange(Lq, dtype=attn.dtype), 1.0)
        attn = attn / row_counts[None, :, None]
        ctx = jnp.einsum('blm,bmd->bld', attn, v)
        return ctx @ Wo.T

    def _L0_ffn_ref(x, Wq_pk, pk_keys, Wq, keys_table, values_table, Wo):
        import jax, jax.numpy as jnp
        import numpy as np
        DIM = 64
        HEADS = 8
        NUM_KEYS = 64
        NUM_KV = NUM_KEYS ** 2
        PK_TOPK = 16
        FINAL_TOPK = 16
        DIM_KEY = DIM // 2
        P = 2

        def _pk(x, Wq_pk, pk_keys):
            b, n, _ = x.shape
            q = (x @ Wq_pk).reshape(b, n, P, HEADS, DIM_KEY).transpose(2, 0, 1, 3, 4)
            sim = jnp.einsum('pbnhd,pkhd->pbnhk', q, pk_keys)
            scores, idx = jax.lax.top_k(sim, PK_TOPK)
            idx0 = idx[0]
            idx1 = idx[1] * NUM_KEYS
            index = (idx0[..., :, None] + idx1[..., None, :]).reshape(b, n, HEADS, PK_TOPK * PK_TOPK)
            score = (scores[0][..., :, None] + scores[1][..., None, :]).reshape(b, n, HEADS, PK_TOPK * PK_TOPK)
            final_scores, pk_idx = jax.lax.top_k(score, FINAL_TOPK)
            final_indices = jnp.take_along_axis(index, pk_idx, axis=-1)
            final_scores = jax.nn.softmax(final_scores, axis=-1)
            return (final_scores, final_indices)
        b, n, d = x.shape
        q = (x @ Wq).reshape(b, n, HEADS, DIM) * DIM ** (-0.5)
        kv_scores, indices = _pk(x, Wq_pk, pk_keys)
        offsets = jnp.arange(HEADS, dtype=indices.dtype) * NUM_KV
        ind = indices + offsets[None, None, :, None]
        k = jnp.einsum('bnhk,bnhkd->bnhd', kv_scores, keys_table[ind])
        v = jnp.einsum('bnhk,bnhkd->bnhd', kv_scores, values_table[ind])
        sim = jnp.einsum('bihd,bjhd->bhij', q, k)
        neg = -jnp.finfo(sim.dtype).max
        causal = jnp.tril(jnp.ones((n, n), dtype=bool))
        sim = jnp.where(causal, sim, neg)
        attn = jax.nn.softmax(sim, axis=-1)
        out = jnp.einsum('bhij,bjhd->bhid', attn, v)
        out = out.transpose(0, 2, 1, 3).reshape(b, n, HEADS * DIM)
        return out @ Wo
    h = _L0_tok_ref(x, L0_tok_fc0_w, L0_tok_fc0_b, L0_tok_ln0_g, L0_tok_ln0_b, L0_tok_w1r, L0_tok_w1i, L0_tok_w2r, L0_tok_w2i, L0_tok_conv_w, L0_tok_conv_b, L0_tok_ln_g, L0_tok_ln_b, L0_tok_fc1_w, L0_tok_fc1_b, L0_tok_fc2_w, L0_tok_fc2_b, L0_tok_fc3_w, L0_tok_fc3_b)
    h = _layernorm(h + _L0_attn_ref(h, L0_attn_Wq, L0_attn_Wk, L0_attn_Wv, L0_attn_Wo), axis=-1)
    h = _layernorm(h + _L0_ffn_ref(h, L0_ffn_Wq_pk, L0_ffn_pk_keys, L0_ffn_Wq, L0_ffn_keys_table, L0_ffn_values_table, L0_ffn_Wo), axis=-1)
    return h

_drawn_inputs = setup_inputs


def setup_inputs(seed=0):
    import zlib

    import numpy as np

    out = dict(_drawn_inputs(seed))
    spreads = {'L0_tok_fc0_b': (0.0, 0.1),
     'L0_tok_ln0_g': (1.0, 0.2),
     'L0_tok_ln0_b': (0.0, 0.1),
     'L0_tok_conv_b': (0.0, 0.1),
     'L0_tok_ln_g': (1.0, 0.2),
     'L0_tok_ln_b': (0.0, 0.1),
     'L0_tok_fc1_b': (0.0, 0.1),
     'L0_tok_fc2_b': (0.0, 0.1)}
    factors = {'L0_tok_w1r': 8.0,
     'L0_tok_w1i': 55.854,
     'L0_tok_w2r': 54.516,
     'L0_tok_w2i': 55.641,
     'L0_attn_Wq': 8.0,
     'L0_attn_Wk': 8.0,
     'L0_attn_Wv': 8.0,
     'L0_attn_Wo': 8.0,
     'L0_ffn_Wq_pk': 8.0,
     'L0_ffn_pk_keys': 8.0,
     'L0_ffn_Wq': 64.0,
     'L0_ffn_keys_table': 64.0,
     'L0_ffn_values_table': 8.0,
     'L0_ffn_Wo': 8.0}
    for name, (base, spread) in spreads.items():
        noise = np.random.default_rng([zlib.crc32(name.encode()), seed]).standard_normal(out[name].shape)
        drawn = base * np.exp(spread * noise) if base else spread * noise
        out[name] = jnp.asarray(drawn.astype(out[name].dtype))
    for name, factor in factors.items():
        out[name] = (out[name] * factor).astype(out[name].dtype)
    return out
```

```python
from contextlib import ExitStack

import numpy as np

import concourse.bass as bass
from concourse import mybir
from concourse.alu_op_type import AluOpType as ALU

F32 = mybir.dt.float32
I32 = mybir.dt.int32
U32 = mybir.dt.uint32
ACT = mybir.ActivationFunctionType
AX = mybir.AxisListType

B, H, W, CH = 64, 64, 64, 3
WIDTH, LAYERS, M1, M2N = 32, 4, 12, 12
NKX, NKY = 2 * M1, M2N
GROUPS = 4
QUADS = 4
STEPS = 32
STAGES = LAYERS + 1
PX = H * W
BANK = 512
P = 128
EPS = 1e-5
MAGIC = 1597463007.0

LAG_T1, LAG_T2, LAG_W = 6, 7, 9
NR = 13

A_STEP = STEPS + 3 * QUADS
B_STEP = STEPS
N_F3, N_MIX, N_TS, N_HI, N_T3 = 12, 18, 6, 12, 16
A_F3, B_F3 = A_STEP, B_STEP
A_MIX, B_MIX = A_F3 + N_F3 // 2, B_F3 + N_F3 // 2
A_TS, B_TS = A_MIX + N_MIX // 2, B_MIX + N_MIX // 2
A_HI, B_HI = A_TS + N_TS // 2, B_TS + N_TS // 2
A_T3, B_T3 = A_HI + N_HI // 2, B_HI + N_HI // 2
A_FWD, B_FWD = A_T3 + N_T3 // 2, B_T3 + N_T3 // 2
A_FC, B_FC = 6 * STEPS, STEPS
A_GROUP, B_GROUP = LAYERS * A_FWD + A_FC, LAYERS * B_FWD + B_FC
CHUNKS, CH_MODES = 9, 8


def a_wdft(i):
    return i + 3 * (i // 8)


def a_tc(q, k):
    return 8 * (q + 1) + 3 * q + k


def a_fc1(i, k):
    return 4 * i + k + 2 * max(i - 1, 0)


def a_fc2(i, k):
    return 4 * min(i + 2, STEPS) + 2 * i + k


def pixels(ap, quad, step):
    r = step % 8
    start = quad * PX + (8 * (r // 2) + r % 2) * P
    return [ap[:, start + 2 * P * j:start + 2 * P * j + P] for j in range(4)]


def pixel_run(ap, quad, step):
    r = step % 8
    half = ap[:, quad * PX + 8 * (r // 2) * P:quad * PX + 8 * (r // 2 + 1) * P]
    return half.rearrange("p (j f x) -> p f j x", f=2, x=P)[:, r % 2]


def build(nc, c, d, hs, out):
    sb = lambda n, s, t=F32: c.enter_context(nc.sbuf_tensor(n, s, t))
    sem = lambda n: c.enter_context(nc.semaphore(n))
    psum = c.enter_context(nc.psum_tensor("psum", [P, 8 * BANK], F32))
    bank = lambda n: psum[:, n * BANK:(n + 1) * BANK]
    y_bank, t_bank, a_bank, b_bank = [bank(0), bank(1)], [bank(2), bank(3)], [bank(4), bank(5)], [bank(6), bank(7)]

    h = sb("h", [P, QUADS * PX])
    yz = sb("yz", [P, 8 * BANK])
    sq = sb("sq", [P, 2 * BANK])
    ssq = sb("ssq", [P, 2 * 64])
    rs = sb("rs", [P, 2 * 64])
    rt = sb("rt", [P, 2 * 64])
    pl = sb("pl", [P, 2 * BANK])
    cw = sb("cw", [P, 2 * NKY * P])
    dk = sb("dk", [P, 16 * NKY * WIDTH])
    ci = dk
    xg = sb("xg", [P, QUADS * 2048])
    XPAD = 72 * 64 + 64
    xs = xg[:, 0:XPAD]
    m2 = xg[:, XPAD:XPAD + 3 * 16 * 48]
    gi = xg
    ss = cw[0:96, :]
    wm = sb("wm", [P, 3 * 2048])

    cst = sb("cst", [P, d["consts"].shape[1]])
    off = 0

    def take(n):
        nonlocal off
        off += n
        return cst[:, off - n:off]

    ident, fw, fh, fhi, fwi, cbd = take(128), take(96), take(96), take(256), take(256), take(128)
    convT, fc0T = take(4 * 128), take(16)
    fc1z, fc2w, fc3w = take(512), take(64), take(32)
    cols = take(4)
    fc1_b, fc2_b, fc3_b = cols[:, 0:1], cols[:, 1:2], cols[:, 2:3]
    lnc = sb("lnc", [P, 2])
    dcc, dcs = sb("dcc", [32, 4]), sb("dcs", [32, 1])
    wconv = sb("wconv", [P, 4 * 128])
    wx = sb("wx", [P, 128])
    z1, z2 = dk[:, 0:4096], dk[:, 4096:6144]
    o3 = sb("o3", [64, 2 * BANK])

    s_const, s_init, s_prep, s_prepc = sem("s_const"), sem("s_init"), sem("s_prep"), sem("s_prepc")
    s_y, s_sq, s_ssq, s_nr, s_z, s_t1, s_h = (sem("s_y"), sem("s_sq"), sem("s_ssq"), sem("s_nr"), sem("s_z"),
                                             sem("s_t1"), sem("s_h"))
    s_aF, s_aD, s_bF, s_bD = sem("s_aF"), sem("s_aD"), sem("s_bF"), sem("s_bD")
    s_x = [sem("s_x0"), sem("s_x1")]
    s_w = [sem("s_w0"), sem("s_w1"), sem("s_w2")]
    s_wfree = sem("s_wfree")
    s_dc, s_ln, s_dcc = sem("s_dc"), sem("s_ln"), sem("s_dcc")
    s_out = [sem("s_out0"), sem("s_out1")]

    used = [0, 0]

    def mem(n):
        k = 0 if used[0] + n <= QUADS * PX else 1
        used[k] += n
        return (h, dk)[k][:, used[k] - n:used[k]]

    ffn = Ffn(nc, c, d, hs.rearrange("b (r w) -> (b r) w", w=W), out, mem, bank(3))
    block = c.enter_context(nc.Block())

    @block.sync
    def _(sp):
        sp.dma_start(cst[:, :], d["consts"]).then_inc(s_const, 16)
        sp.wait_ge(s_init, 1)
        def layer_norm(g, st):
            sp.wait_ge(s_h, g * (STAGES * STEPS) + st * STEPS)
            sp.dma_start(lnc[:, :], d["ln"][bass.ds(st * P, P), 0:2]).then_inc(s_ln, 16)

        def conv_bias(g, st):
            sp.wait_ge(s_h, g * (STAGES * STEPS) + st * STEPS + 1)
            sp.dma_start(dcc[:, :], d["ln"][bass.ds(st * P, 32), :]).then_inc(s_dcc, 16)

        def load_x(g, q):
            sp.wait_ge(s_y, g * (STAGES * STEPS) + (0 if q < 2 else 8 * (q - 1)))
            slot = xg[:, (q % 2) * PX:(q % 2) * PX + PX]
            sp.dma_start(slot[0:12, :], d["x"][bass.ds(g * 48 + q * 12, 12), :]).then_inc(s_x[q % 2], 16)
            sp.dma_start(slot[12:13, :], d["ones"]).then_inc(s_x[q % 2], 16)

        def modes(g, st):
            for k in range(CHUNKS):
                sp.wait_ge(s_wfree, g * (LAYERS * CHUNKS) + st * CHUNKS + k + 1)
                sp.dma_start(wm[:, (k % 3) * 2048:(k % 3 + 1) * 2048],
                             d["modes"][bass.ds(st * (CHUNKS * P) + k * P, P), :]).then_inc(s_w[k % 3], 16)

        with sp.Fori(0, GROUPS) as g:
            load_x(g, 0)
            load_x(g, 1)
            layer_norm(g, 0)
            load_x(g, 2)
            conv_bias(g, 0)
            load_x(g, 3)
            modes(g, 0)
            with sp.Fori(1, LAYERS) as l:
                layer_norm(g, l)
                conv_bias(g, l)
                modes(g, l)
            layer_norm(g, LAYERS)
            for i in range(STEPS):
                q, r = i // 8, i % 8
                s, e = q // 2, q % 2
                sp.wait_ge(s_bD, g * B_GROUP + LAYERS * B_FWD + i + 1)
                for p2 in range(2):
                    for a in range(2):
                        dst = hs[bass.ds(g * 16 + 8 * s + 4 * p2 + 2 * a + e, 1),
                                 8 * (r // 2) * P:8 * (r // 2 + 1) * P]
                        dst = dst.rearrange("p (j f x) -> p f j x", f=2, x=P)[:, r % 2]
                        src = o3[32 * p2 + a:32 * p2 + a + 1, (i % 2) * BANK:(i % 2 + 1) * BANK]
                        sp.dma_start(dst, src.rearrange("p (j x) -> p j x", x=P)).then_inc(s_out[i % 2], 16)
        for k in range(2):
            sp.wait_ge(s_out[k], GROUPS * (STEPS // 2) * 64)
        sp.dma_start(ffn.cst, d["consts2"]).then_inc(ffn.s_const, 16)
        with sp.Fori(0, GROUPS) as g:
            for kind, j in ffn.order:
                if kind == "hT":
                    ffn.sp_load(sp, g, j)
                if kind == "res2":
                    ffn.sp_store(sp, g, j)
        for k in range(2):
            sp.wait_ge(ffn.s_store[k], GROUPS * (TILES // 2) * 16)

    @block.gpsimd
    def _(pool):
        with pool.Fori(0, GROUPS) as g:
            for kind, j in ffn.order:
                if kind.startswith("unit"):
                    ffn.pool_unit(pool, g, j, int(kind[4:]))

    @block.tensor
    def _(pe):
        mm = nc.tensor.matmul
        pe.wait_ge(s_const, 16)
        for l in range(4):
            mm(bank(0)[:, l * P:(l + 1) * P], convT[:, l * P:(l + 1) * P], cbd, start=True, stop=True)
        mm(bank(1)[0:16, 0:P], fc0T, cbd, start=True, stop=True).then_inc(s_prep, 1)
        for _ in range(3):
            last = mm(bank(2)[:, 0:P], ident, ident, start=True, stop=True)
            last.then_inc(s_wfree, 1)
        pe.wait_ge(s_prepc, 2)

        def free(done, base, at, full):
            if at >= 2:
                pe.wait_ge(done, base + at - 1)

        def stage(kind, sg, l, ab, bb, xbase, wbase):
            def y_step(i):
                q, r = i // 8, i % 8
                if i >= 2:
                    pe.wait_ge(s_sq, sg + i - 1)
                y = y_bank[i % 2]
                if kind == "first":
                    if r == 0:
                        pe.wait_ge(s_x[q % 2], xbase + 32 * (q // 2 + 1))
                    for j, blk in enumerate(pixels(xg, q % 2, i)):
                        last = mm(y[:, j * P:(j + 1) * P], blk, wx[:, :], start=True, stop=True)
                else:
                    if r == 0:
                        pe.wait_ge(s_aD, ab + A_T3 - A_FWD + 2 * (q + 1))
                        pe.wait_ge(s_bD, bb + B_T3 - B_FWD + 2 * (q + 1))
                    at = q * 2048 + (r // 2) * BANK
                    w = wconv[:, bass.ds(l * P, P)] if not isinstance(l, int) else wconv[:, l * P:(l + 1) * P]
                    for j, blk in enumerate(pixels(h, q, i)):
                        mm(y[:, j * P:(j + 1) * P], blk, w, start=(j == 0), stop=False, skip_group_check=True)
                    last = mm(y, fwi[0:96, (r % 2) * P:(r % 2 + 1) * P], gi[0:96, at:at + BANK],
                              start=False, stop=True, skip_group_check=True)
                last.then_inc(s_y, 1)

            def t1_step(i):
                pe.wait_ge(s_z, sg + i + 1)
                if i >= 2:
                    pe.wait_ge(s_h, sg + i - 1)
                z = yz[:, (i % 8) * BANK:(i % 8 + 1) * BANK]
                for j in range(4):
                    last = nc.tensor.transpose(t_bank[i % 2][:, j * P:(j + 1) * P], z[:, j * P:(j + 1) * P], ident)
                last.then_inc(s_t1, 1)

            def t2_step(i):
                pe.wait_ge(s_h, sg + i + 1)
                free(s_bD, bb, i, s_bF)
                for j, blk in enumerate(pixels(h, i // 8, i)):
                    last = nc.tensor.transpose(b_bank[i % 2][:, j * P:(j + 1) * P], blk, ident)
                last.then_inc(s_bF, 1)

            def w_step(i):
                at = a_wdft(i)
                pe.wait_ge(s_bD, bb + i + 1)
                free(s_aD, ab, at, s_aF)
                p = pl[:, (i % 2) * BANK:(i % 2 + 1) * BANK]
                for j in range(4):
                    last = mm(a_bank[at % 2][:, j * 96:(j + 1) * 96], p[:, j * P:(j + 1) * P], fw, start=True, stop=True)
                last.then_inc(s_aF, 1)

            def tc_step(q, k):
                at = a_tc(q, k)
                if k == 0:
                    pe.wait_ge(s_aD, ab + a_wdft(8 * q + 7) + 1)
                else:
                    free(s_aD, ab, at, s_aF)
                for j in range(4):
                    src = cw[:, (q % 2) * NKY * P + (4 * k + j) * P:(q % 2) * NKY * P + (4 * k + j + 1) * P]
                    last = nc.tensor.transpose(a_bank[at % 2][:, j * P:(j + 1) * P], src, ident)
                last.then_inc(s_aF, 1)

            def fc1_step(i):
                pe.wait_ge(s_h, sg + i + 1)
                for k in range(4):
                    at = a_fc1(i, k)
                    free(s_aD, ab, at, s_aF)
                    mm(a_bank[at % 2], fc1z[:, k * P:(k + 1) * P], pixel_run(h, i // 8, i),
                       start=True, stop=True).then_inc(s_aF, 1)

            def fc2_step(i):
                for k in range(2):
                    at = a_fc2(i, k)
                    pe.wait_ge(s_aD, ab + max(at - 1, a_fc1(i, 2 * k + 1) + 1))
                    for m in range(2):
                        src = z1[:, (i % 2) * 2048 + (2 * k + m) * BANK:(i % 2) * 2048 + (2 * k + m + 1) * BANK]
                        last = mm(a_bank[at % 2][64 * m:64 * m + 64, :], fc2w, src, start=True, stop=True)
                    last.then_inc(s_aF, 1)

            def fc3_step(i):
                pe.wait_ge(s_aD, ab + a_fc2(i, 1) + 1)
                free(s_bD, bb, i, s_bF)
                for k in range(2):
                    src = z2[:, (i % 2) * 1024 + k * BANK:(i % 2) * 1024 + (k + 1) * BANK]
                    last = mm(b_bank[i % 2][32 * k:32 * k + 32, :], fc3w, src, start=True, stop=True)
                last.then_inc(s_bF, 1)

            if kind == "last":
                for i in range(STEPS + LAG_T2 + 2):
                    if i < STEPS:
                        y_step(i)
                    if 0 <= i - LAG_T1 < STEPS:
                        t1_step(i - LAG_T1)
                    if 0 <= i - LAG_T2 < STEPS:
                        fc1_step(i - LAG_T2)
                    if 0 <= i - LAG_T2 - 1 < STEPS:
                        fc2_step(i - LAG_T2 - 1)
                    if 0 <= i - LAG_T2 - 2 < STEPS:
                        fc3_step(i - LAG_T2 - 2)
                return
            for i in range(STEPS + LAG_W):
                if i < STEPS:
                    y_step(i)
                if 0 <= i - LAG_T1 < STEPS:
                    t1_step(i - LAG_T1)
                if 0 <= i - LAG_T2 < STEPS:
                    t2_step(i - LAG_T2)
                if 0 <= i - LAG_W < STEPS:
                    w_step(i - LAG_W)
                    if (i - LAG_W) % 8 == 7:
                        for k in range(3):
                            tc_step((i - LAG_W) // 8, k)
            pe.wait_ge(s_aD, ab + A_F3)

            def ring(n, a0, b0):
                if n % 2 == 0:
                    at, full, done, base, banks = a0 + n // 2, s_aF, s_aD, ab, a_bank
                else:
                    at, full, done, base, banks = b0 + n // 2, s_bF, s_bD, bb, b_bank
                pe.wait_ge(done, base + at - 1)
                return banks[at % 2], full

            for n in range(N_F3):
                out, full = ring(n, A_F3, B_F3)
                for m in range(4):
                    at = (4 * (n % 4) + m) * NKY * WIDTH + (n // 4) * P
                    last = mm(out[:, m * 96:(m + 1) * 96], dk[:, at:at + P], fh, start=True, stop=True)
                last.then_inc(full, 1)
            pe.wait_ge(s_aD, ab + A_MIX)
            pe.wait_ge(s_bD, bb + B_MIX)
            for n in range(N_MIX):
                if n % 2 == 0:
                    k = n // 2
                    pe.wait_ge(s_w[k % 3], wbase + 16 * (k // 3 + 1))
                out, full = ring(n, A_MIX, B_MIX)
                for m in range(4):
                    w0 = (n // 2 % 3) * 2048 + ((n % 2) * 4 + m) * 256
                    x0 = (4 * n + m) * 64
                    for ri in range(2):
                        last = mm(out[:, m * 96:(m + 1) * 96], wm[:, w0 + ri * P:w0 + (ri + 1) * P],
                                  xs[:, x0 + 32 * ri:x0 + 32 * ri + 96], start=(ri == 0), stop=(ri == 1))
                last.then_inc(full, 1)
                if n % 2 == 1:
                    mm(t_bank[0][:, 0:P], ident, ident, start=True, stop=True).then_inc(s_wfree, 1)
            pe.wait_ge(s_aD, ab + A_TS)
            pe.wait_ge(s_bD, bb + B_TS)
            for n in range(N_TS):
                out, full = ring(n, A_TS, B_TS)
                for m in range(4):
                    at = (n // 2) * 768 + (4 * (n % 2) + m) * 96
                    last = mm(out[0:96, m * P:(m + 1) * P], m2[:, at:at + 96], cbd, start=True, stop=True)
                last.then_inc(full, 1)
            pe.wait_ge(s_aD, ab + A_HI)
            pe.wait_ge(s_bD, bb + B_HI)
            for n in range(N_HI):
                out, full = ring(n, A_HI, B_HI)
                for s in range(2):
                    last = mm(out[:, s * 256:(s + 1) * 256], ss[:, n * 256 + s * P:n * 256 + (s + 1) * P],
                              fhi[0:96, :], start=True, stop=True)
                last.then_inc(full, 1)
            pe.wait_ge(s_aD, ab + A_T3)
            pe.wait_ge(s_bD, bb + B_T3)
            for n in range(N_T3):
                out, full = ring(n, A_T3, B_T3)
                for m in range(4):
                    at = (n // 4) * 1536 + (4 * (n % 4) + m) * 96
                    last = nc.tensor.transpose(out[0:96, m * P:(m + 1) * P], ci[:, at:at + 96], ident)
                last.then_inc(full, 1)

        with pe.Fori(0, GROUPS) as g:
            sg, ab, bb, wb = g * (STAGES * STEPS), g * A_GROUP, g * B_GROUP, g * (LAYERS * 48)
            stage("first", sg, None, ab, bb, g * 64, wb)
            with pe.Fori(0, LAYERS - 1) as l:
                stage("mid", sg + STEPS + l * STEPS, l, ab + A_FWD + l * A_FWD, bb + B_FWD + l * B_FWD, None,
                      wb + 48 + l * 48)
            stage("last", sg + 4 * STEPS, 3, ab + 4 * A_FWD, bb + 4 * B_FWD, None, None)
        pe.wait_ge(ffn.s_const, 16)
        with pe.Fori(0, GROUPS) as g:
            for kind, j in ffn.order:
                ffn.pe_event(pe, g, kind, j)

    @block.scalar
    def _(act):
        A = nc.scalar.activation
        act.wait_ge(s_prep, 1)
        A(wconv[:, :], bank(0), ACT.Identity).then_inc(s_prepc, 1)

        def stage(kind, sg, l, ab, bb, dcb):
            def sq_step(i):
                act.wait_ge(s_y, sg + i + 1)
                if i >= 2:
                    act.wait_ge(s_ssq, sg + i - 1)
                A(sq[:, (i % 2) * BANK:(i % 2 + 1) * BANK], y_bank[i % 2], ACT.Square, scale=WIDTH ** -0.5)
                if i >= 8:
                    act.wait_ge(s_t1, sg + i - 7)
                A(yz[:, (i % 8) * BANK:(i % 8 + 1) * BANK], y_bank[i % 2], ACT.Identity).then_inc(s_sq, 1)

            def h_step(i):
                act.wait_ge(s_t1, sg + i + 1)
                fn = ACT.Gelu if kind == "mid" else ACT.Identity
                if i == 0:
                    act.wait_ge(s_ln, 16 * stage.index + 16)
                A(pixel_run(h, i // 8, i), t_bank[i % 2].rearrange("p (j x) -> p j x", x=P), fn,
                  scale=lnc[:, 0:1], bias=lnc[:, 1:2]).then_inc(s_h, 1)

            def w_step(i):
                at = a_wdft(i)
                act.wait_ge(s_aF, ab + at + 1)
                r, q = i % 8, i // 8
                dst = cw[:, (q % 2) * NKY * P:(q % 2 + 1) * NKY * P].rearrange(
                    "p (k u j f x) -> p u f j k x", k=NKY, u=4, j=4, f=2)[:, r // 2, r % 2]
                src = a_bank[at % 2][:, 0:384].rearrange("p (j z) -> p j z", z=96)[:, :, 0:48].rearrange(
                    "p j (k x) -> p j k x", x=4)
                A(dst, src, ACT.Identity).then_inc(s_aD, 1)

            def tc_step(q, k):
                at = a_tc(q, k)
                act.wait_ge(s_aF, ab + at + 1)
                s, e = q // 2, q % 2
                dst = dk[:, s * 8 * 384:(s + 1) * 8 * 384].rearrange(
                    "p (g e k c) -> p e g k c", g=4, e=2, k=NKY)[:, e, :, 4 * k:4 * k + 4, :]
                src = a_bank[at % 2].rearrange("p (k g c) -> p g k c", k=4, g=4)
                A(dst, src, ACT.Identity).then_inc(s_aD, 1)

            if kind == "last":
                for i in range(STEPS + LAG_T2 + 1):
                    if i < STEPS:
                        sq_step(i)
                    if 0 <= i - LAG_T1 < STEPS:
                        h_step(i - LAG_T1)
                    n = i - LAG_T2
                    if 0 <= n < STEPS:
                        for k in range(4):
                            at = a_fc1(n, k)
                            act.wait_ge(s_aF, ab + at + 1)
                            A(z1[:, (n % 2) * 2048 + k * BANK:(n % 2) * 2048 + (k + 1) * BANK], a_bank[at % 2],
                              ACT.Gelu, bias=fc1_b).then_inc(s_aD, 1)
                    n -= 1
                    if 0 <= n < STEPS:
                        for k in range(2):
                            at = a_fc2(n, k)
                            act.wait_ge(s_aF, ab + at + 1)
                            if n >= 2:
                                act.wait_ge(s_bF, bb + n - 1)
                            A(z2[:, (n % 2) * 1024 + k * BANK:(n % 2) * 1024 + (k + 1) * BANK], a_bank[at % 2],
                              ACT.Gelu, bias=fc2_b).then_inc(s_aD, 1)
                return
            for i in range(STEPS + LAG_W):
                if i < STEPS:
                    sq_step(i)
                if 0 <= i - LAG_T1 < STEPS:
                    h_step(i - LAG_T1)
                if 0 <= i - LAG_W < STEPS:
                    w_step(i - LAG_W)
                    if (i - LAG_W) % 8 == 7:
                        for k in range(3):
                            tc_step((i - LAG_W) // 8, k)

            def even(total, a0):
                for n in range(0, total, 2):
                    act.wait_ge(s_aF, ab + a0 + n // 2 + 1)
                    yield n, a_bank[(a0 + n // 2) % 2]

            for n, src in even(N_F3, A_F3):
                A(f3_dst(xs, n), f3_src(src), ACT.Identity).then_inc(s_aD, 1)
            for n, src in even(N_MIX, A_MIX):
                done = A(mix_dst(m2, n), mix_src(src), ACT.Identity)
                if n == 0:
                    done.then_inc(s_dc, 1)
                    act.wait_ge(s_dcc, 16 * dcb + 16)
                    A(dcs[:, :], dcc[:, 2:3], ACT.Identity, scale=float(PX)).then_inc(s_dc, 1)
                    act.wait_ge(s_dc, 2 * dcb + 2)
                    done = A(m2[0:32, 0:768].rearrange("p (m z) -> p m z", z=48)[:, :, 0], src[0:32, 0:16],
                             ACT.Identity, bias=dcs[:, :])
                done.then_inc(s_aD, 1)
            for n, src in even(N_TS, A_TS):
                A(ts_dst(ss, n), ts_src(src), ACT.Identity).then_inc(s_aD, 1)
            for n, src in even(N_HI, A_HI):
                A(hi_dst(ci, n), hi_src(src), ACT.Identity).then_inc(s_aD, 1)
            for n, src in even(N_T3, A_T3):
                A(gi[0:96, n * BANK:(n + 1) * BANK], src[0:96, :], ACT.Identity).then_inc(s_aD, 1)

        with act.Fori(0, GROUPS) as g:
            sg, ab, bb = g * (STAGES * STEPS), g * A_GROUP, g * B_GROUP
            stage.index = g * STAGES
            stage("first", sg, 0, ab, bb, g * LAYERS)
            with act.Fori(1, LAYERS) as l:
                stage.index = g * STAGES + l
                stage("mid", sg + l * STEPS, l, ab + l * A_FWD, bb + l * B_FWD, g * LAYERS + l)
            stage.index = g * STAGES + LAYERS
            stage("last", sg + 4 * STEPS, 4, ab + 4 * A_FWD, bb + 4 * B_FWD, None)
        act.wait_ge(ffn.s_const, 16)
        with act.Fori(0, GROUPS) as g:
            for kind, j in ffn.order:
                ffn.act_event(act, g, kind, j)

    @block.vector
    def _(dve):
        V = nc.vector
        V.memset(xg[:, :], 0.0).then_inc(s_init, 1)
        V.memset(wx[:, :], 0.0).then_inc(s_init, 1)
        dve.wait_ge(s_init, 2)
        dve.wait_ge(s_prep, 1)
        V.tensor_copy(wx[0:13, :], bank(1)[0:13, 0:P]).then_inc(s_prepc, 1)

        def stage(kind, sg, ab, bb):
            def sum_step(i):
                dve.wait_ge(s_sq, sg + i + 1)
                b = (i // 4) % 2
                if i % 4 == 0 and i >= 8:
                    dve.wait_ge(s_z, sg + i - 4)
                V.tensor_reduce(ssq[:, b * 64 + (i % 4) * 16:b * 64 + (i % 4 + 1) * 16],
                                sq[:, (i % 2) * BANK:(i % 2 + 1) * BANK].rearrange("p (a c) -> p a c", c=WIDTH),
                                AX.X, ALU.add).then_inc(s_ssq, 1)

            def rsqrt_batch(n):
                nb = sg // 4 * NR if isinstance(sg, int) else None
                base = nrb(sg, n)
                half = slice((n % 2) * 64, (n % 2 + 1) * 64)
                v, y, t = ssq[:, half], rs[:, half], rt[:, half]
                k = 0

                def link(ins):
                    nonlocal k
                    k += 1
                    ins.then_inc(s_nr, 1)
                    dve.wait_ge(s_nr, base + k)

                dve.wait_ge(s_ssq, sg + 4 * n + 4)
                link(V.tensor_scalar(v, v, EPS, None, ALU.add))
                link(V.tensor_scalar(t.bitcast(I32), v.bitcast(I32), 1, None, ALU.logical_shift_right))
                link(V.tensor_scalar(y.bitcast(I32), t.bitcast(I32), -1.0, MAGIC, ALU.mult, ALU.add))
                for _ in range(3):
                    link(V.scalar_tensor_tensor(t, y, -0.5, y, ALU.mult, ALU.mult))
                    link(V.tensor_tensor(t, t, v, ALU.mult))
                    link(V.scalar_tensor_tensor(y, t, 1.5, y, ALU.add, ALU.mult))
                link(V.tensor_copy(t, y))
                assert k == NR

            def z_step(i):
                z = yz[:, (i % 8) * BANK:(i % 8 + 1) * BANK].rearrange("p (a c) -> p a c", c=WIDTH)
                b = (i // 4) % 2
                r = rs[:, b * 64 + (i % 4) * 16:b * 64 + (i % 4 + 1) * 16].unsqueeze(2).broadcast_to([P, 16, WIDTH])
                V.tensor_tensor(z, z, r, ALU.mult).then_inc(s_z, 1)

            def t2_step(i):
                dve.wait_ge(s_bF, bb + i + 1)
                if i >= 2:
                    dve.wait_ge(s_aF, ab + a_wdft(i - 2) + 1)
                V.tensor_copy(pl[:, (i % 2) * BANK:(i % 2 + 1) * BANK], b_bank[i % 2]).then_inc(s_bD, 1)

            def fc3_step(i):
                dve.wait_ge(s_bF, bb + i + 1)
                dve.wait_ge(s_out[i % 2], outb + 64 * (i // 2))
                V.tensor_scalar(o3[:, (i % 2) * BANK:(i % 2 + 1) * BANK], b_bank[i % 2][0:64, :], fc3_b[0:64, :],
                                None, ALU.add).then_inc(s_bD, 1)

            lag3 = LAG_T2 + 2 if kind == "last" else LAG_T2
            outb = stage.outb
            for i in range(STEPS + lag3 + 1):
                if i < STEPS:
                    sum_step(i)
                if i < STEPS and i % 4 == 3:
                    rsqrt_batch(i // 4)
                if 0 <= i - 4 < STEPS:
                    z_step(i - 4)
                if 0 <= i - lag3 < STEPS:
                    (fc3_step if kind == "last" else t2_step)(i - lag3)
            if kind == "last":
                return

            def odd(total, b0):
                for n in range(1, total, 2):
                    dve.wait_ge(s_bF, bb + b0 + n // 2 + 1)
                    yield n, b_bank[(b0 + n // 2) % 2]

            for n, src in odd(N_F3, B_F3):
                V.tensor_copy(f3_dst(xs, n), f3_src(src)).then_inc(s_bD, 1)
            for n, src in odd(N_MIX, B_MIX):
                V.tensor_copy(mix_dst(m2, n), mix_src(src)).then_inc(s_bD, 1)
            for n, src in odd(N_TS, B_TS):
                V.tensor_copy(ts_dst(ss, n), ts_src(src)).then_inc(s_bD, 1)
            for n, src in odd(N_HI, B_HI):
                V.tensor_copy(hi_dst(ci, n), hi_src(src)).then_inc(s_bD, 1)
            for n, src in odd(N_T3, B_T3):
                V.tensor_copy(gi[0:96, n * BANK:(n + 1) * BANK], src[0:96, :]).then_inc(s_bD, 1)

        with dve.Fori(0, GROUPS) as g:
            sg, ab, bb = g * (STAGES * STEPS), g * A_GROUP, g * B_GROUP
            nr0 = g * (STAGES * 8 * NR)
            stage.outb = g * (STEPS // 2 * 64)
            nrb = lambda sg_, n: nr0 + n * NR
            stage("first", sg, ab, bb)
            with dve.Fori(1, LAYERS) as l:
                nrb = lambda sg_, n: nr0 + l * (8 * NR) + n * NR
                stage("mid", sg + l * STEPS, ab + l * A_FWD, bb + l * B_FWD)
            nrb = lambda sg_, n: nr0 + (4 * 8 + n) * NR
            stage("last", sg + 4 * STEPS, ab + 4 * A_FWD, bb + 4 * B_FWD)
        dve.wait_ge(ffn.s_const, 16)
        for k in range(2):
            V.memset(ffn.st[:, k:k + 1], 0.0).then_inc(ffn.s_ws, 1)
        with dve.Fori(0, GROUPS) as g:
            ffn.dve_start(dve, g)
            for kind, j in ffn.order:
                ffn.dve_event(dve, g, kind, j)
            assert ffn.vn == ffn.V_GROUP


def f3_dst(xs, n):
    kyg, i4 = n // 4, n % 4
    return xs[:, kyg * 1536:(kyg + 1) * 1536].rearrange("p (z m) -> p m z", m=16)[:, 4 * i4:4 * i4 + 4, :]


def f3_src(bank):
    return bank[:, 0:384].rearrange("p (m z) -> p m z", m=4)


def mix_dst(m2, n):
    kyg, k4 = n // 6, n % 6
    return m2[:, kyg * 768:(kyg + 1) * 768].rearrange("p (m k r) -> p k r m", m=16, k=24)[:, 4 * k4:4 * k4 + 4]


def mix_src(bank):
    return bank[:, 0:384].rearrange("p (k z) -> p k z", k=4)[:, :, 0:32].rearrange("p k (r m) -> p k r m", r=2)


def ts_dst(ss, n):
    kyg, s = n // 2, n % 2
    return ss[:, kyg * 1024:(kyg + 1) * 1024].rearrange("p (k s g c) -> p s g k c", k=4, s=2, g=4)[:, s]


def ts_src(bank):
    return bank[0:96, :].rearrange("p (g k c) -> p g k c", g=4, k=4)


def hi_dst(ci, n):
    return ci[:, :].rearrange("p (q h k r) -> p k q h r", q=4, h=64, k=12)[:, n]


def hi_src(bank):
    return bank.rearrange("p (q h r) -> p q h r", q=4, r=2)


def dft_constants():
    kx = np.array(list(range(M1)) + list(range(H - M1, H)))
    w = np.arange(W)
    ident = np.eye(P)
    fw = np.zeros((2, W, NKY, 2, 2))
    fh = np.zeros((H, 2, NKX, 4))
    fhi = np.zeros((2, NKX, 2, 2, H, 2))
    fwi = np.zeros((4, NKY, 2, 2, 2, W))
    for k in range(NKY):
        a = 2 * np.pi * k * w / W
        for r in range(2):
            fw[r, :, k, r, 0] = np.cos(a)
            fw[r, :, k, r, 1] = -np.sin(a)
            for f in range(2):
                fwi[2 * f + r, k, 0, f, r] = np.cos(a) * (2 if k else 1) / W
                fwi[2 * f + r, k, 1, f, r] = -np.sin(a) * (2 if k else 0) / W
    a = 2 * np.pi * np.outer(np.arange(H), kx) / H
    for v, (re, im) in enumerate(((np.cos(a), np.sin(a)), (-np.sin(a), np.cos(a)),
                                  (np.sin(a), -np.cos(a)), (np.cos(a), np.sin(a)))):
        fh[:, 0, :, v] = re
        fh[:, 1, :, v] = im
    for e in range(2):
        fhi[e, :, 0, e, :, 0] = np.cos(a.T) / H
        fhi[e, :, 0, e, :, 1] = np.sin(a.T) / H
        fhi[e, :, 1, e, :, 0] = -np.sin(a.T) / H
        fhi[e, :, 1, e, :, 1] = np.cos(a.T) / H
    cbd = np.kron(np.eye(4), np.eye(WIDTH) - 1.0 / WIDTH)
    pad = lambda m, n: np.concatenate([m, np.zeros((P - m.shape[0], n))], 0) if m.shape[0] < P else m
    fwp = np.zeros((P, 96))
    fwp[:, 0:48] = fw.reshape(P, 48)
    return [ident, fwp, fh.reshape(P, 96), pad(fhi.reshape(96, 256), 256), pad(fwi.reshape(96, 256), 256), cbd]


def lay_out(a):
    f = np.float32
    get = lambda n: np.asarray(a["L0_tok_" + n])
    x = np.asarray(a["x"]).reshape(4, 2, 4, 2, PX, CH).transpose(0, 1, 3, 2, 5, 4).reshape(4 * 4 * 12, PX)
    w = np.stack([np.concatenate([get("w1" + r), get("w2" + r)], 3) for r in "ri"])
    w = w.reshape(2, LAYERS, WIDTH, WIDTH, NKX, 3, 4).transpose(1, 6, 2, 5, 4, 0, 3)
    modes = np.zeros((LAYERS, CHUNKS, 4, WIDTH, CH_MODES, 2, 4, WIDTH), f)
    w = w.reshape(LAYERS, 4, WIDTH, CHUNKS, CH_MODES, 2, WIDTH)
    for k in range(4):
        modes[:, :, k, :, :, :, k, :] = w[:, k].transpose(0, 2, 1, 3, 4, 5)
    consts = [m.astype(f) for m in dft_constants()]
    conv = np.zeros((4, WIDTH, LAYERS, 4, WIDTH), f)
    fc0 = np.zeros((4, WIDTH, 16), f)
    fc1 = np.zeros((4, WIDTH, 4, P), f)
    fc3 = np.zeros((2, 64, 32), f)
    for g in range(4):
        conv[g, :, :, g, :] = get("conv_w").transpose(1, 0, 2)
        fc0[g, :, 3 * g:3 * g + 3] = get("fc0_w").T
        fc0[g, :, 12] = get("fc0_b")
        fc1[g, :, g, :] = get("fc1_w")
    for g in range(2):
        fc3[g, :, g] = get("fc3_w")[:, 0]
    cols = np.zeros((P, 4), f)
    cols[:, 0] = get("fc1_b")
    cols[:, 1] = np.tile(get("fc2_b"), 2)
    cols[:, 2] = get("fc3_b")[0]
    ln = np.zeros((STAGES, P, 4), f)
    ln[0, :, 0], ln[0, :, 1] = np.tile(get("ln0_g"), 4), np.tile(get("ln0_b"), 4)
    ln[1:, :, 0], ln[1:, :, 1] = np.tile(get("ln_g"), (1, 4)), np.tile(get("ln_b"), (1, 4))
    ln[0:LAYERS, 0:32, 2] = get("conv_b")
    consts += [conv.reshape(P, 512), fc0.reshape(P, 16), fc1.reshape(P, 512), get("fc2_w"), fc3.reshape(P, 32), cols]
    return {"x": np.ascontiguousarray(x), "ones": np.ones((1, PX), f),
            "ln": ln.reshape(STAGES * P, 4), "modes": modes.reshape(LAYERS * CHUNKS * P, 2048), "consts": np.concatenate(consts, 1)}


TILE = P
TILES = 8
HEADS, NK, TOPK, DIM = 8, 64, 16, 64
ROWS_AB = [(0, 1, 16), (1, 1, 8), (2, 1, 5), (3, 1, 4), (4, 1, 3), (5, 3, 2), (8, 8, 1)]
CELLS = sum(r * n for _, r, n in ROWS_AB)
NEG = -3.0e38
PRE = ["hT", "qkv", "att", "ctx", "res1", "h1T", "qpk", "sim0", "sim1"]
POST = ["qT", "kT", "s0", "pT0", "o0", "s1", "pT1", "o1", "oT", "res2"]
JOBS = PRE + POST
PREP_NR = 11


def schedule():
    order = []
    for j in range(TILES + 2):
        pre = [(n, j) for n in PRE + ["select"]] if j < TILES else []
        post = [(n, j - 2) for n in POST] if j >= 2 else []
        units = [("unit%d" % u, j - 1) for u in range(HEADS)] if 1 <= j <= TILES else []
        lists = [post, pre, units]
        slots = max(len(x) for x in lists)
        for k in range(slots):
            for x in lists:
                lo, hi = k * len(x) // slots, (k + 1) * len(x) // slots
                order += x[lo:hi]
    return order


def ring_index(order):
    jobs = [e for e in order if e[0] in JOBS]
    return {e: n for n, e in enumerate(jobs)}, len(jobs)


class Ffn:

    def __init__(self, nc, c, d, hs, out, mem, bank):
        self.nc = nc
        self.d, self.hs, self.out, self.bank = d, hs, out, bank
        sem = lambda n: c.enter_context(nc.semaphore(n))
        cst = mem(d["consts2"].shape[1])
        self.cst = cst
        off = 0

        def take(n):
            nonlocal off
            off += n
            return cst[:, off - n:off]

        self.ident, self.wqpk, self.wq, self.keys, self.wo = take(128), take(512), take(512), take(1024), take(256)
        self.aw = take(256)
        self.mask1, self.mask2, self.hoff, self.iota = take(128), take(128), take(128), take(CELLS)
        self.gb = mem(2 * 2048)
        self.hin = mem(2 * 64)
        self.hT, self.qk, self.v1, self.att, self.ctx = mem(128), mem(256), mem(64), mem(128), mem(128)
        self.h1, self.h1T = mem(4 * 64), mem(4 * 128)
        self.st = mem(16)
        self.qpk, self.sims = mem(512), mem(512)
        self.top, self.ti = mem(256), mem(256)
        self.jf = mem(256)
        self.cand, self.cidx = mem(HEADS * CELLS), mem(HEADS * CELLS)
        self.cv, self.cp, self.cpf = mem(128), mem(128), mem(128)
        self.oh = mem(2 * TOPK * CELLS)
        self.fi, self.iu, self.wt = mem(128), mem(2 * 128), mem(2 * 128)
        self.wsum = mem(16)
        self.kv = mem(2 * 1024)
        self.kT, self.qT, self.s, self.pT, self.o, self.oT = mem(512), mem(512), mem(512), mem(512), mem(512), mem(512)
        self.nmax, self.psum_, self.prec = mem(8), mem(8), mem(8)
        self.res = mem(2 * 64)
        self.s_const = sem("s_const2")
        self.s_hin = [sem("s_hin0"), sem("s_hin1")]
        self.s_fF, self.s_fD = sem("s_fF"), sem("s_fD")
        self.s_v = sem("s_v")
        self.s_top = sem("s_top")
        self.s_sub, self.s_exp = sem("s_sub"), sem("s_exp")
        self.s_idx = sem("s_idx")
        self.s_gath = [sem("s_gath%d" % i) for i in range(4)]
        self.s_ws = sem("s_ws")
        self.s_res1 = sem("s_res1")
        self.s_mx, self.s_p = sem("s_mx"), sem("s_p")
        self.s_o = sem("s_o")
        self.s_fin = sem("s_fin")
        self.s_store = [sem("s_store0"), sem("s_store1")]
        self.order = schedule()
        self.at, self.njobs = ring_index(self.order)

    def sp_load(self, sp, g, j):
        t = g * TILES + j
        if j >= 2:
            sp.wait_ge(self.s_res1, t - 1)
        sp.dma_start(self.hin[:, (j % 2) * 64:(j % 2 + 1) * 64],
                     self.hs[bass.ds(t * TILE, TILE), :]).then_inc(self.s_hin[j % 2], 16)

    def sp_store(self, sp, g, j):
        t = g * TILES + j
        sp.wait_ge(self.s_fin, t + 1)
        sp.dma_start(self.out[bass.ds(t * TILE, TILE), :],
                     self.res[:, (j % 2) * 64:(j % 2 + 1) * 64]).then_inc(self.s_store[j % 2], 16)

    def settled(self, engine):
        engine.nop(nofuse=True)

    def pool_unit(self, pool, g, j, u):
        t, n = g * TILES + j, 8 * j + u
        if u == 0:
            pool.wait_ge(self.s_idx, t + 1)
        unit = g * (TILES * HEADS) + n
        pool.wait_ge(self.s_ws, unit + 1)
        self.settled(pool)
        for k in range(TOPK):
            at = (n % 2) * 2048 + k * 128
            col = (j % 2) * 128 + u * TOPK + k
            self.nc.gpsimd.indirect_dma_start(
                out=self.gb[:, at:at + 128], out_offset=None, in_=self.d["kv"],
                in_offset=bass.IndirectOffsetOnAxis(ap=self.iu[:, col:col + 1].bitcast(U32), axis=0),
            ).then_inc(self.s_gath[n % 4], 16)

    def pe_event(self, pe, g, kind, j):
        if kind not in JOBS:
            return
        nc, mm = self.nc, self.nc.tensor.matmul
        f = g * self.njobs + self.at[(kind, j)]
        b = self.bank
        t = g * TILES + j
        pe.wait_ge(self.s_fD, f)
        if kind == "qkv":
            self.settled(pe)
        h1T = self.h1T[:, (j % 4) * 128:(j % 4 + 1) * 128]
        kk = self.kv[:, (j % 2) * 1024:(j % 2) * 1024 + 512]
        vv = self.kv[:, (j % 2) * 1024 + 512:(j % 2 + 1) * 1024]
        if kind == "hT":
            pe.wait_ge(self.s_hin[j % 2], g * (TILES // 2 * 16) + 16 * (j // 2 + 1))
            self.settled(pe)
            last = nc.tensor.transpose(b[0:64, 0:P], self.hin[:, (j % 2) * 64:(j % 2 + 1) * 64], self.ident)
        elif kind == "qkv":
            mm(b[0:64, 0:P], self.aw[0:64, 0:64], self.hT[0:64, :], start=True, stop=True)
            mm(b[0:64, P:2 * P], self.aw[0:64, 64:128], self.hT[0:64, :], start=True, stop=True)
            last = mm(b[:, 2 * P:2 * P + 64], self.hT[0:64, :], self.aw[0:64, 128:192], start=True, stop=True)
        elif kind == "att":
            last = mm(b[:, 0:P], self.qk[0:64, P:2 * P], self.qk[0:64, 0:P], start=True, stop=True)
        elif kind == "ctx":
            last = mm(b[0:64, 0:P], self.v1, self.att, start=True, stop=True)
        elif kind == "res1":
            last = mm(b[:, 0:64], self.ctx[0:64, :], self.aw[0:64, 192:256], start=True, stop=True)
        elif kind == "h1T":
            pe.wait_ge(self.s_res1, t + 1)
            self.settled(pe)
            last = nc.tensor.transpose(b[0:64, 0:P], self.h1[:, (j % 4) * 64:(j % 4 + 1) * 64], self.ident)
        elif kind == "qpk":
            for m in range(4):
                last = mm(b[:, m * P:(m + 1) * P], self.wqpk[0:64, m * P:(m + 1) * P], h1T[0:64, :],
                          start=True, stop=True)
        elif kind in ("sim0", "sim1"):
            p = int(kind[3])
            for m in range(2):
                last = mm(b[:, m * 256:(m + 1) * 256], self.qpk[:, (2 * p + m) * P:(2 * p + m + 1) * P],
                          self.keys[:, (2 * p + m) * 256:(2 * p + m + 1) * 256], start=True, stop=True)
        elif kind == "qT":
            for m in range(4):
                last = mm(b[:, m * P:(m + 1) * P], self.wq[0:64, m * P:(m + 1) * P], h1T[0:64, :],
                          start=True, stop=True)
        elif kind == "kT":
            pe.wait_ge(self.s_ws, (t + 1) * HEADS + 2)
            for m in range(4):
                last = nc.tensor.transpose(b[:, m * P:(m + 1) * P], kk[:, m * P:(m + 1) * P], self.ident)
        elif kind in ("s0", "s1"):
            hf = int(kind[1])
            for m in range(4):
                rows, col = slice(64 * hf, 64 * hf + 64), slice(m * P, (m + 1) * P)
                last = mm(b[:, m * P:(m + 1) * P], self.qT[rows, col], self.kT[rows, col], start=True, stop=True)
        elif kind in ("pT0", "pT1"):
            pe.wait_ge(self.s_p, 2 * t + int(kind[2]) + 1)
            for m in range(4):
                last = nc.tensor.transpose(b[:, m * P:(m + 1) * P], self.s[:, m * P:(m + 1) * P], self.ident)
        elif kind in ("o0", "o1"):
            for m in range(4):
                hd = 2 * m + int(kind[1])
                last = mm(b[:, m * 64:(m + 1) * 64], self.pT[:, m * P:(m + 1) * P], vv[:, hd * 64:(hd + 1) * 64],
                          start=True, stop=True)
        elif kind == "oT":
            for m in range(4):
                last = nc.tensor.transpose(b[:, m * P:(m + 1) * P], self.o[:, m * P:(m + 1) * P], self.ident)
        elif kind == "res2":
            for m in range(4):
                last = mm(b[:, 0:64], self.oT[:, m * P:(m + 1) * P], self.wo[:, m * 64:(m + 1) * 64],
                          start=(m == 0), stop=(m == 3))
        last.then_inc(self.s_fF, 1)

    def act_event(self, act, g, kind, j):
        A = self.nc.scalar.activation
        f = None
        if kind in JOBS:
            f = g * self.njobs + self.at[(kind, j)]
        t = g * TILES + j
        b = self.bank
        h1T = self.h1T[:, (j % 4) * 128:(j % 4 + 1) * 128]
        plain = {"hT": (self.hT[0:64, :], b[0:64, 0:P]), "ctx": (self.ctx[0:64, :], b[0:64, 0:P]),
                 "h1T": (h1T[0:64, :], b[0:64, 0:P]), "qpk": (self.qpk, b), "kT": (self.kT, b),
                 "sim0": (self.sims, b), "sim1": (self.sims, b), "pT0": (self.pT, b), "pT1": (self.pT, b),
                 "oT": (self.oT, b)}
        if kind in plain:
            act.wait_ge(self.s_fF, f + 1)
            if kind in ("sim0", "sim1"):
                act.wait_ge(self.s_top, 2 * t + int(kind[3]))
            A(plain[kind][0], plain[kind][1], ACT.Identity).then_inc(self.s_fD, 1)
        elif kind == "qkv":
            act.wait_ge(self.s_fF, f + 1)
            A(self.qk[0:64, :], b[0:64, 0:2 * P], ACT.Identity)
            A(self.v1, b[:, 2 * P:2 * P + 64], ACT.Identity).then_inc(self.s_fD, 1)
        elif kind == "qT":
            act.wait_ge(self.s_fF, f + 1)
            A(self.qT, b, ACT.Identity, scale=DIM ** -0.5).then_inc(self.s_fD, 1)
        elif kind == "select":
            act.wait_ge(self.s_sub, t + 1)
            w = self.wt[:, (j % 2) * 128:(j % 2 + 1) * 128]
            A(w, w, ACT.Exp).then_inc(self.s_exp, 1)
        elif kind in ("s0", "s1"):
            act.wait_ge(self.s_mx, 2 * t + int(kind[1]) + 1)
            for m in range(4):
                hd = 4 * int(kind[1]) + m
                last = A(self.s[:, m * P:(m + 1) * P], self.s[:, m * P:(m + 1) * P], ACT.Exp,
                         bias=self.nmax[:, hd:hd + 1], accum_out=self.psum_[:, hd:hd + 1])
            last.then_inc(self.s_p, 1)

    def dve_start(self, dve, g):
        self.vn = 0
        self.vbase = g * self.V_GROUP

    def link(self, dve, ins):
        self.vn += 1
        ins.then_inc(self.s_v, 1)
        dve.wait_ge(self.s_v, self.vbase + self.vn)

    V_GROUP = 71 * TILES

    def layer_norm(self, dve, src, dst, done):
        V, st = self.nc.vector, self.st
        mv, v, y, t = st[:, 6:8], st[:, 7:8], st[:, 8:9], st[:, 9:10]
        L = lambda ins: self.link(dve, ins)
        L(V.bn_stats(st[:, 0:6], src))
        self.settled(dve)
        L(V.bn_aggr(mv, st[:, 0:6]))
        L(V.tensor_scalar(v, v, EPS, None, ALU.add))
        L(V.tensor_scalar(t.bitcast(I32), v.bitcast(I32), 1, None, ALU.logical_shift_right))
        L(V.tensor_scalar(y.bitcast(I32), t.bitcast(I32), -1.0, MAGIC, ALU.mult, ALU.add))
        for _ in range(3):
            L(V.scalar_tensor_tensor(t, y, -0.5, y, ALU.mult, ALU.mult))
            L(V.tensor_tensor(t, t, v, ALU.mult))
            L(V.scalar_tensor_tensor(y, t, 1.5, y, ALU.add, ALU.mult))
        V.tensor_scalar(dst, src, mv[:, 0:1], y, ALU.subtract, ALU.mult).then_inc(done, 1)

    def top16(self, dve, src, vals, idx, seg):
        V = self.nc.vector
        for r in range(2):
            sl = lambda x, h: x[:, h * 16 + 8 * r:h * 16 + 8 * r + 8]
            for h in range(HEADS):
                last = V.max(sl(vals, h), src[:, h * seg:(h + 1) * seg])
            self.link(dve, last)
            self.settled(dve)
            for h in range(HEADS):
                last = V.max_index(sl(idx, h).bitcast(U32), sl(vals, h), src[:, h * seg:(h + 1) * seg])
            self.link(dve, last)
            self.settled(dve)
            if r == 0:
                for h in range(HEADS):
                    x = src[:, h * seg:(h + 1) * seg]
                    last = V.match_replace(x, sl(vals, h), x, NEG)
                self.link(dve, last)
                self.settled(dve)

    def dve_event(self, dve, g, kind, j):
        nc, V = self.nc, self.nc.vector
        f = g * self.njobs + self.at[(kind, j)] if kind in JOBS else None
        t = g * TILES + j
        b = self.bank
        link = lambda ins: self.link(dve, ins)
        h1 = self.h1[:, (j % 4) * 64:(j % 4 + 1) * 64]
        kv = self.kv[:, (j % 2) * 1024:(j % 2 + 1) * 1024].rearrange("p (w h x) -> p w h x", w=2, h=HEADS)
        w = self.wt[:, (j % 2) * 128:(j % 2 + 1) * 128]
        if kind == "att":
            dve.wait_ge(self.s_fF, f + 1)
            V.scalar_tensor_tensor(self.att, b[:, 0:P], 0.0, self.mask1, ALU.max, ALU.mult).then_inc(self.s_fD, 1)
        elif kind == "res1":
            dve.wait_ge(self.s_fF, f + 1)
            ins = V.tensor_tensor(h1, self.hin[:, (j % 2) * 64:(j % 2 + 1) * 64], b[:, 0:64], ALU.add)
            ins.then_inc(self.s_fD, 1)
            dve.wait_ge(self.s_fD, f + 1)
            self.layer_norm(dve, h1, h1, self.s_res1)
        elif kind in ("sim0", "sim1"):
            dve.wait_ge(self.s_fD, f + 1)
            p = int(kind[3])
            self.settled(dve)
            self.top16(dve, self.sims, self.top[:, 128 * p:128 * (p + 1)], self.ti[:, 128 * p:128 * (p + 1)], NK)
            V.tensor_copy(self.jf[:, 128 * p:128 * (p + 1)],
                          self.ti[:, 128 * p:128 * (p + 1)].bitcast(U32)).then_inc(self.s_top, 1)
        elif kind == "select":
            dve.wait_ge(self.s_top, 2 * t + 2)
            j1 = self.jf[:, 128:256]
            link(V.scalar_tensor_tensor(j1, j1, float(NK), self.hoff, ALU.mult, ALU.add))
            for x, y in ((self.top, self.cand), (self.jf, self.cidx)):
                c3 = y[:, :].rearrange("p (h n) -> p h n", h=HEADS)
                x0 = x[:, 0:128].rearrange("p (h n) -> p h n", h=HEADS)
                x1 = x[:, 128:256].rearrange("p (h n) -> p h n", h=HEADS)
                at = 0
                for a, rows, n in ROWS_AB:
                    o = c3[:, :, at:at + rows * n]
                    if rows == 1:
                        i0, i1 = x0[:, :, a:a + 1].broadcast_to([P, HEADS, n]), x1[:, :, 0:n]
                    elif n == 1:
                        i0, i1 = x0[:, :, a:a + rows], x1[:, :, 0:1].broadcast_to([P, HEADS, rows])
                    else:
                        o = o.rearrange("p h (r n) -> p h r n", r=rows)
                        i0 = x0[:, :, a:a + rows].unsqueeze(3).broadcast_to([P, HEADS, rows, n])
                        i1 = x1[:, :, 0:n].unsqueeze(2).broadcast_to([P, HEADS, rows, n])
                    last = V.tensor_tensor(o, i0, i1, ALU.add)
                    at += rows * n
            link(last)
            self.settled(dve)
            self.top16(dve, self.cand, self.cv, self.cp, CELLS)
            v3 = self.cv[:, :].rearrange("p (h n) -> p h n", h=HEADS)
            w3 = w.rearrange("p (h n) -> p h n", h=HEADS)
            V.tensor_tensor(w3, v3, v3[:, :, 0:1].broadcast_to([P, HEADS, TOPK]), ALU.subtract).then_inc(self.s_sub, 1)
            link(V.tensor_copy(self.cpf, self.cp.bitcast(U32)))
            for h2 in range(0, HEADS, 2):
                sh = [P, 2, TOPK, CELLS]
                oh = self.oh[:, :].rearrange("p (h k n) -> p h k n", h=2, k=TOPK)
                pos = self.cpf[:, h2 * TOPK:(h2 + 2) * TOPK].rearrange("p (h k) -> p h k", h=2)
                ohf = self.oh[:, :].rearrange("p (x n) -> p x n", n=CELLS)
                link(V.tensor_tensor(ohf, self.cpf[:, h2 * TOPK:(h2 + 2) * TOPK].unsqueeze(2).broadcast_to(
                    [P, 2 * TOPK, CELLS]), self.iota.unsqueeze(1).broadcast_to([P, 2 * TOPK, CELLS]), ALU.is_equal))
                ci = self.cidx[:, h2 * CELLS:(h2 + 2) * CELLS].rearrange("p (h n) -> p h n", h=2)
                link(V.tensor_tensor(oh, oh, ci.unsqueeze(2).broadcast_to(sh), ALU.mult))
                link(V.tensor_reduce(self.fi[:, h2 * TOPK:(h2 + 2) * TOPK], ohf, AX.X, ALU.add))
            V.tensor_copy(self.iu[:, (j % 2) * 128:(j % 2 + 1) * 128].bitcast(U32), self.fi).then_inc(self.s_idx, 1)
            dve.wait_ge(self.s_exp, t + 1)
            link(V.tensor_reduce(self.wsum[:, 0:8], w3, AX.X, ALU.add))
            link(V.reciprocal(self.wsum[:, 8:16], self.wsum[:, 0:8]))
            link(V.tensor_tensor(w3, w3, self.wsum[:, 8:16].unsqueeze(2).broadcast_to([P, HEADS, TOPK]), ALU.mult))
        elif kind.startswith("unit"):
            u = int(kind[4:])
            n = 8 * j + u
            dve.wait_ge(self.s_gath[n % 4], g * (TILES * HEADS // 4 * 256) + 256 * (n // 4 + 1))
            rows = self.gb[:, (n % 2) * 2048:(n % 2 + 1) * 2048].rearrange("p (k x) -> p k x", k=TOPK)
            wu = w[:, u * TOPK:(u + 1) * TOPK].unsqueeze(2).broadcast_to([P, TOPK, 128])
            link(V.tensor_tensor(rows, rows, wu, ALU.mult))
            V.tensor_reduce(kv[:, :, u, :], rows.rearrange("p k (w x) -> p w x k", w=2), AX.X,
                            ALU.add).then_inc(self.s_ws, 1)
        elif kind in ("s0", "s1"):
            dve.wait_ge(self.s_fF, f + 1)
            hf = int(kind[1])
            s3 = self.s[:, :].rearrange("p (h n) -> p h n", h=4)
            V.tensor_tensor(s3, b.rearrange("p (h n) -> p h n", h=4),
                            self.mask2.unsqueeze(1).broadcast_to([P, 4, P]), ALU.add).then_inc(self.s_fD, 1)
            dve.wait_ge(self.s_fD, f + 1)
            V.tensor_reduce(self.nmax[:, 4 * hf:4 * hf + 4], s3, AX.X, ALU.max, negate=True).then_inc(self.s_mx, 1)
        elif kind in ("o0", "o1"):
            hf = int(kind[1])
            dve.wait_ge(self.s_fF, f + 1)
            link(V.reciprocal(self.prec[:, 4 * hf:4 * hf + 4], self.psum_[:, 4 * hf:4 * hf + 4]))
            V.tensor_tensor(self.o[:, :].rearrange("p (m f x) -> p f m x", m=4, f=2)[:, hf],
                            b[:, 0:256].rearrange("p (h x) -> p h x", h=4),
                            self.prec[:, 4 * hf:4 * hf + 4].unsqueeze(2).broadcast_to([P, 4, 64]),
                            ALU.mult).then_inc(self.s_fD, 1)
        elif kind == "res2":
            dve.wait_ge(self.s_fF, f + 1)
            res = self.res[:, (j % 2) * 64:(j % 2 + 1) * 64]
            dve.wait_ge(self.s_store[j % 2], g * (TILES // 2 * 16) + 16 * (j // 2))
            V.tensor_tensor(res, h1, b[:, 0:64], ALU.add).then_inc(self.s_fD, 1)
            dve.wait_ge(self.s_fD, f + 1)
            self.layer_norm(dve, res, res, self.s_fin)


def lay_out_ffn(a):
    f = np.float32
    aw = np.concatenate([np.asarray(a["L0_attn_W" + n]).T for n in "qkvo"], 1)
    pad = lambda m: np.concatenate([m, np.zeros((P - m.shape[0], m.shape[1]), f)], 0)
    keys = np.zeros((2, 2, 4, 32, 4, NK), f)
    pk = np.asarray(a["L0_ffn_pk_keys"]).transpose(0, 2, 3, 1).reshape(2, 2, 4, 32, NK)
    for m in range(4):
        keys[:, :, m, :, m, :] = pk[:, :, m]
    keys = keys.reshape(4, P, 256).transpose(1, 0, 2).reshape(P, 1024)
    wo = np.asarray(a["L0_ffn_Wo"]).reshape(4, P, DIM).transpose(1, 0, 2).reshape(P, 256)
    i = np.arange(P)
    same = (i[:, None] // 64) == (i[None, :] // 64)
    mask1 = np.where(same & (i[:, None] <= i[None, :]), 1.0 / np.maximum(i % 64, 1)[None, :], 0.0).astype(f)
    mask2 = np.where(same & (i[None, :] <= i[:, None]), 0.0, NEG).astype(f)
    hoff = np.broadcast_to(np.repeat(np.arange(HEADS) * NK * NK, TOPK).astype(f), (P, 128))
    iota = np.broadcast_to(np.arange(CELLS).astype(f), (P, CELLS))
    return {"consts2": np.concatenate([np.eye(P, dtype=f), pad(np.asarray(a["L0_ffn_Wq_pk"])),
                                       pad(np.asarray(a["L0_ffn_Wq"])), keys, wo, pad(aw), mask1, mask2, hoff, iota], 1),
            "kv": np.concatenate([np.asarray(a["L0_ffn_keys_table"]), np.asarray(a["L0_ffn_values_table"])], 1)}



def kernel(**inputs):
    import concourse.bacc as bacc
    from concourse.bass_utils import run_bass_kernel_spmd

    arrays = {**lay_out(inputs), **lay_out_ffn(inputs)}
    nc = bacc.Bacc("TRN2", target_bir_lowering=False, num_devices=1)
    arrays = {"in_" + n: np.ascontiguousarray(a) for n, a in arrays.items()}
    d = {n[3:]: nc.dram_tensor(n, a.shape, mybir.dt.from_np(a.dtype), kind="ExternalInput").ap()
         for n, a in arrays.items()}
    hs = nc.dram_tensor("tower", (B, PX), F32, kind="Internal").ap()
    out = nc.dram_tensor("out_0", (B * H, W), F32, kind="ExternalOutput").ap()
    with ExitStack() as c:
        build(nc, c, d, hs, out)
    r = run_bass_kernel_spmd(nc, [arrays], core_ids=[0])
    return r.results[0]["out_0"].reshape(B, H, W)
```

```python
from contextlib import ExitStack

import numpy as np

import concourse.bass as bass
from concourse import mybir
from concourse.alu_op_type import AluOpType as ALU

F32 = mybir.dt.float32
I32 = mybir.dt.int32
U32 = mybir.dt.uint32
ACT = mybir.ActivationFunctionType
AX = mybir.AxisListType

B, H, W, CH = 64, 64, 64, 3
WIDTH, LAYERS, M1, M2N = 32, 4, 12, 12
NKX, NKY = 2 * M1, M2N
GROUPS = 4
QUADS = 4
STEPS = 32
STAGES = LAYERS + 1
PX = H * W
BANK = 512
P = 128
EPS = 1e-5
MAGIC = 1597463007.0

LAG_T1, LAG_T2, LAG_W = 6, 7, 9
NR = 13

A_STEP = STEPS + 3 * QUADS
B_STEP = STEPS
N_F3, N_MIX, N_TS, N_HI, N_T3 = 12, 18, 6, 12, 16
A_F3, B_F3 = A_STEP, B_STEP
A_MIX, B_MIX = A_F3 + N_F3 // 2, B_F3 + N_F3 // 2
A_TS, B_TS = A_MIX + N_MIX // 2, B_MIX + N_MIX // 2
A_HI, B_HI = A_TS + N_TS // 2, B_TS + N_TS // 2
A_T3, B_T3 = A_HI + N_HI // 2, B_HI + N_HI // 2
A_FWD, B_FWD = A_T3 + N_T3 // 2, B_T3 + N_T3 // 2
A_FC, B_FC = 6 * STEPS, STEPS
A_GROUP, B_GROUP = LAYERS * A_FWD + A_FC, LAYERS * B_FWD + B_FC
CHUNKS, CH_MODES = 18, 4

STAGE_UNITS = 8
LOOP_PIECES = 11

LOOP_EVERY = {"first": 3, "mid": 3, "last": 2}


def a_wdft(i):
    return i + 3 * (i // 8)


def a_tc(q, k):
    return 8 * (q + 1) + 3 * q + k


def a_fc1(i, k):
    return 4 * i + k + 2 * max(i - 1, 0)


def a_fc2(i, k):
    return 4 * min(i + 2, STEPS) + 2 * i + k


def pixels(ap, quad, step):
    r = step % 8
    start = quad * PX + (8 * (r // 2) + r % 2) * P
    return [ap[:, start + 2 * P * j:start + 2 * P * j + P] for j in range(4)]


def pixel_run(ap, quad, step):
    r = step % 8
    half = ap[:, quad * PX + 8 * (r // 2) * P:quad * PX + 8 * (r // 2 + 1) * P]
    return half.rearrange("p (j f x) -> p f j x", f=2, x=P)[:, r % 2]


def build(nc, c, d, hs, kvd, out):
    sb = lambda n, s, t=F32: c.enter_context(nc.sbuf_tensor(n, s, t))
    sem = lambda n: c.enter_context(nc.semaphore(n))
    psum = c.enter_context(nc.psum_tensor("psum", [P, 8 * BANK], F32))
    bank = lambda n: psum[:, n * BANK:(n + 1) * BANK]
    y_bank, t_bank, a_bank, b_bank = [bank(0), bank(1)], [bank(2), bank(3)], [bank(4), bank(5)], [bank(6), bank(7)]

    h = sb("h", [P, QUADS * PX])
    yz = sb("yz", [P, 8 * BANK])
    sq = sb("sq", [P, 2 * BANK])
    ssq = sb("ssq", [P, 2 * 64])
    rs = sb("rs", [P, 2 * 64])
    rt = sb("rt", [P, 2 * 64])
    pl = sb("pl", [P, 2 * BANK])
    cw = sb("cw", [P, 2 * NKY * P])
    dk = sb("dk", [P, 16 * NKY * WIDTH])
    ci = dk
    xg = sb("xg", [P, QUADS * 2048])
    XPAD = 72 * 64 + 64
    xs = xg[:, 0:XPAD]
    m2 = xg[:, XPAD:XPAD + 3 * 16 * 48]
    gi = xg
    ss = cw[0:96, :]
    wm = sb("wm", [P, 3 * 1024])

    cst = sb("cst", [P, d["consts"].shape[1]])
    off = 0

    def take(n):
        nonlocal off
        off += n
        return cst[:, off - n:off]

    ident, fw, fh, fhi, fwi, cbd = take(128), take(96), take(96), take(256), take(256), take(128)
    convT, fc0T = h[:, 0:512], h[:, 512:528]
    fc1z, fc2w, fc3w = take(512), take(64), take(32)
    cols = take(4)
    fc1_b, fc2_b, fc3_b = cols[:, 0:1], cols[:, 1:2], cols[:, 2:3]
    lnc = sb("lnc", [P, 2])
    dcc, dcs = sb("dcc", [32, 4]), sb("dcs", [32, 1])
    wconv = sb("wconv", [P, 4 * 128])
    wx = sb("wx", [P, 128])
    z1, z2 = dk[:, 0:4096], dk[:, 4096:6144]
    o3 = pl[0:64, :]

    s_const, s_init, s_prep, s_prepc = sem("s_const"), sem("s_init"), sem("s_prep"), sem("s_prepc")
    s_y, s_sq, s_ssq, s_nr, s_z, s_t1, s_h = (sem("s_y"), sem("s_sq"), sem("s_ssq"), sem("s_nr"), sem("s_z"),
                                             sem("s_t1"), sem("s_h"))
    s_aF, s_aD, s_bF, s_bD = sem("s_aF"), sem("s_aD"), sem("s_bF"), sem("s_bD")
    s_x = [sem("s_x0"), sem("s_x1")]
    s_w = [sem("s_w0"), sem("s_w1"), sem("s_w2")]
    s_wfree = sem("s_wfree")
    s_dc, s_ln, s_dcc = sem("s_dc"), sem("s_ln"), sem("s_dcc")
    s_out = [sem("s_out0"), sem("s_out1")]

    keep = lambda n: sb("keep%d" % len(kept), [P, kept.append(n) or n])[:, :]
    kept = []
    used = [0]

    def mem(n):
        used[0] += n
        return h[:, used[0] - n:used[0]]

    ffn = Ffn(nc, c, d, hs.rearrange("b (r w) -> (b r) w", w=W), kvd, out, keep, mem, bank(3))
    block = c.enter_context(nc.Block())

    @block.sync
    def _(sp):
        sp.dma_start(cst[:, :], d["consts"]).then_inc(s_const, 16)
        sp.dma_start(h[:, 0:528], d["setup"]).then_inc(s_const, 16)
        sp.wait_ge(s_init, 1)
        def layer_norm(g, st):
            sp.wait_ge(s_h, g * (STAGES * STEPS) + st * STEPS)
            sp.dma_start(lnc[:, :], d["ln"][bass.ds(st * P, P), 0:2]).then_inc(s_ln, 16)

        def conv_bias(g, st):
            sp.wait_ge(s_h, g * (STAGES * STEPS) + st * STEPS + 1)
            sp.dma_start(dcc[:, :], d["ln"][bass.ds(st * P, 32), :]).then_inc(s_dcc, 16)

        def load_x(g, q):
            sp.wait_ge(s_y, g * (STAGES * STEPS) + (0 if q < 2 else 8 * (q - 1)))
            slot = xg[:, (q % 2) * PX:(q % 2) * PX + PX]
            sp.dma_start(slot[0:12, :], d["x"][bass.ds(g * 48 + q * 12, 12), :]).then_inc(s_x[q % 2], 16)
            sp.dma_start(slot[12:13, :], d["ones"]).then_inc(s_x[q % 2], 16)

        def modes(g, st):
            for k in range(CHUNKS):
                sp.wait_ge(s_wfree, g * (LAYERS * CHUNKS) + st * CHUNKS + k + 1)
                sp.dma_start(wm[:, (k % 3) * 1024:(k % 3 + 1) * 1024],
                             d["modes"][bass.ds(st * (CHUNKS * P) + k * P, P), :]).then_inc(s_w[k % 3], 16)

        def tower(g):
            load_x(g, 0)
            load_x(g, 1)
            layer_norm(g, 0)
            load_x(g, 2)
            conv_bias(g, 0)
            load_x(g, 3)
            modes(g, 0)
            with sp.Fori(1, LAYERS) as l:
                layer_norm(g, l)
                conv_bias(g, l)
                modes(g, l)
            layer_norm(g, LAYERS)
            for i in range(STEPS):
                q, r = i // 8, i % 8
                s, e = q // 2, q % 2
                sp.wait_ge(s_bD, g * B_GROUP + LAYERS * B_FWD + i + 1)
                for p2 in range(2):
                    for a in range(2):
                        dst = hs[bass.ds(g * 16 + 8 * s + 4 * p2 + 2 * a + e, 1),
                                 8 * (r // 2) * P:8 * (r // 2 + 1) * P]
                        dst = dst.rearrange("p (j f x) -> p f j x", f=2, x=P)[:, r % 2]
                        src = o3[32 * p2 + a:32 * p2 + a + 1, (i % 2) * BANK:(i % 2 + 1) * BANK]
                        sp.dma_start(dst, src.rearrange("p (j x) -> p j x", x=P)).then_inc(s_out[i % 2], 16)
            for k in range(2):
                sp.wait_ge(s_out[k], g * (STEPS // 2 * 64) + STEPS // 2 * 64)
                ffn.settled(sp)

        tower(0)
        ffn.sp_between(sp, 0, BETWEEN_FIRST)
        with sp.Fori(1, GROUPS) as g:
            tower(g)
            ffn.sp_between(sp, g, BETWEEN)
        ffn.sp_tail(sp)

    @block.gpsimd
    def _(pool):
        with pool.Fori(0, GROUPS) as g:
            ffn.pool_group(pool, g)

    @block.tensor
    def _(pe):
        mm = nc.tensor.matmul
        pe.wait_ge(s_const, 32)
        for l in range(4):
            mm(bank(0)[:, l * P:(l + 1) * P], convT[:, l * P:(l + 1) * P], cbd, start=True, stop=True)
        mm(bank(1)[0:16, 0:P], fc0T, cbd, start=True, stop=True).then_inc(s_prep, 1)
        for _ in range(3):
            last = mm(bank(2)[:, 0:P], ident, ident, start=True, stop=True)
            last.then_inc(s_wfree, 1)
        pe.wait_ge(s_prepc, 2)

        def free(done, base, at, full):
            if at >= 2:
                pe.wait_ge(done, base + at - 1)

        def stage(kind, sg, l, ab, bb, xbase, wbase):
            def y_step(i):
                q, r = i // 8, i % 8
                if i >= 2:
                    pe.wait_ge(s_sq, sg + i - 1)
                y = y_bank[i % 2]
                if kind == "first":
                    if r == 0:
                        pe.wait_ge(s_x[q % 2], xbase + 32 * (q // 2 + 1))
                    for j, blk in enumerate(pixels(xg, q % 2, i)):
                        last = mm(y[:, j * P:(j + 1) * P], blk, wx[:, :], start=True, stop=True)
                else:
                    if r == 0:
                        pe.wait_ge(s_aD, ab + A_T3 - A_FWD + 2 * (q + 1))
                        pe.wait_ge(s_bD, bb + B_T3 - B_FWD + 2 * (q + 1))
                    at = q * 2048 + (r // 2) * BANK
                    w = wconv[:, bass.ds(l * P, P)] if not isinstance(l, int) else wconv[:, l * P:(l + 1) * P]
                    for j, blk in enumerate(pixels(h, q, i)):
                        mm(y[:, j * P:(j + 1) * P], blk, w, start=(j == 0), stop=False, skip_group_check=True)
                    last = mm(y, fwi[0:96, (r % 2) * P:(r % 2 + 1) * P], gi[0:96, at:at + BANK],
                              start=False, stop=True, skip_group_check=True)
                last.then_inc(s_y, 1)

            def t1_step(i):
                pe.wait_ge(s_z, sg + i + 1)
                if i >= 2:
                    pe.wait_ge(s_h, sg + i - 1)
                z = yz[:, (i % 8) * BANK:(i % 8 + 1) * BANK]
                for j in range(4):
                    last = nc.tensor.transpose(t_bank[i % 2][:, j * P:(j + 1) * P], z[:, j * P:(j + 1) * P], ident)
                last.then_inc(s_t1, 1)

            def t2_step(i):
                pe.wait_ge(s_h, sg + i + 1)
                free(s_bD, bb, i, s_bF)
                for j, blk in enumerate(pixels(h, i // 8, i)):
                    last = nc.tensor.transpose(b_bank[i % 2][:, j * P:(j + 1) * P], blk, ident)
                last.then_inc(s_bF, 1)

            def w_step(i):
                at = a_wdft(i)
                pe.wait_ge(s_bD, bb + i + 1)
                free(s_aD, ab, at, s_aF)
                p = pl[:, (i % 2) * BANK:(i % 2 + 1) * BANK]
                for j in range(4):
                    last = mm(a_bank[at % 2][:, j * 96:(j + 1) * 96], p[:, j * P:(j + 1) * P], fw, start=True, stop=True)
                last.then_inc(s_aF, 1)

            def tc_step(q, k):
                at = a_tc(q, k)
                if k == 0:
                    pe.wait_ge(s_aD, ab + a_wdft(8 * q + 7) + 1)
                else:
                    free(s_aD, ab, at, s_aF)
                for j in range(4):
                    src = cw[:, (q % 2) * NKY * P + (4 * k + j) * P:(q % 2) * NKY * P + (4 * k + j + 1) * P]
                    last = nc.tensor.transpose(a_bank[at % 2][:, j * P:(j + 1) * P], src, ident)
                last.then_inc(s_aF, 1)

            def fc1_step(i):
                pe.wait_ge(s_h, sg + i + 1)
                for k in range(4):
                    at = a_fc1(i, k)
                    free(s_aD, ab, at, s_aF)
                    mm(a_bank[at % 2], fc1z[:, k * P:(k + 1) * P], pixel_run(h, i // 8, i),
                       start=True, stop=True).then_inc(s_aF, 1)

            def fc2_step(i):
                for k in range(2):
                    at = a_fc2(i, k)
                    pe.wait_ge(s_aD, ab + max(at - 1, a_fc1(i, 2 * k + 1) + 1))
                    for m in range(2):
                        src = z1[:, (i % 2) * 2048 + (2 * k + m) * BANK:(i % 2) * 2048 + (2 * k + m + 1) * BANK]
                        last = mm(a_bank[at % 2][64 * m:64 * m + 64, :], fc2w, src, start=True, stop=True)
                    last.then_inc(s_aF, 1)

            def fc3_step(i):
                pe.wait_ge(s_aD, ab + a_fc2(i, 1) + 1)
                free(s_bD, bb, i, s_bF)
                for k in range(2):
                    src = z2[:, (i % 2) * 1024 + k * BANK:(i % 2) * 1024 + (k + 1) * BANK]
                    last = mm(b_bank[i % 2][32 * k:32 * k + 32, :], fc3w, src, start=True, stop=True)
                last.then_inc(s_bF, 1)

            if kind == "last":
                for i in range(STEPS + LAG_T2 + 2):
                    if i < STEPS:
                        y_step(i)
                    if 0 <= i - LAG_T1 < STEPS:
                        t1_step(i - LAG_T1)
                    if 0 <= i - LAG_T2 < STEPS:
                        fc1_step(i - LAG_T2)
                    if 0 <= i - LAG_T2 - 1 < STEPS:
                        fc2_step(i - LAG_T2 - 1)
                    if 0 <= i - LAG_T2 - 2 < STEPS:
                        fc3_step(i - LAG_T2 - 2)
                return
            for i in range(STEPS + LAG_W):
                if i < STEPS:
                    y_step(i)
                if 0 <= i - LAG_T1 < STEPS:
                    t1_step(i - LAG_T1)
                if 0 <= i - LAG_T2 < STEPS:
                    t2_step(i - LAG_T2)
                if 0 <= i - LAG_W < STEPS:
                    w_step(i - LAG_W)
                    if (i - LAG_W) % 8 == 7:
                        for k in range(3):
                            tc_step((i - LAG_W) // 8, k)
            pe.wait_ge(s_aD, ab + A_F3)

            def ring(n, a0, b0):
                if n % 2 == 0:
                    at, full, done, base, banks = a0 + n // 2, s_aF, s_aD, ab, a_bank
                else:
                    at, full, done, base, banks = b0 + n // 2, s_bF, s_bD, bb, b_bank
                pe.wait_ge(done, base + at - 1)
                return banks[at % 2], full

            for n in range(N_F3):
                out, full = ring(n, A_F3, B_F3)
                for m in range(4):
                    at = (4 * (n % 4) + m) * NKY * WIDTH + (n // 4) * P
                    last = mm(out[:, m * 96:(m + 1) * 96], dk[:, at:at + P], fh, start=True, stop=True)
                last.then_inc(full, 1)
            pe.wait_ge(s_aD, ab + A_MIX)
            pe.wait_ge(s_bD, bb + B_MIX)
            for n in range(N_MIX):
                pe.wait_ge(s_w[n % 3], wbase + 16 * (n // 3 + 1))
                out, full = ring(n, A_MIX, B_MIX)
                for m in range(4):
                    w0 = (n % 3) * 1024 + m * 256
                    x0 = (4 * n + m) * 64
                    for ri in range(2):
                        last = mm(out[:, m * 96:(m + 1) * 96], wm[:, w0 + ri * P:w0 + (ri + 1) * P],
                                  xs[:, x0 + 32 * ri:x0 + 32 * ri + 96], start=(ri == 0), stop=(ri == 1))
                last.then_inc(full, 1)
                mm(t_bank[0][:, 0:P], ident, ident, start=True, stop=True).then_inc(s_wfree, 1)
            pe.wait_ge(s_aD, ab + A_TS)
            pe.wait_ge(s_bD, bb + B_TS)
            for n in range(N_TS):
                out, full = ring(n, A_TS, B_TS)
                for m in range(4):
                    at = (n // 2) * 768 + (4 * (n % 2) + m) * 96
                    last = mm(out[0:96, m * P:(m + 1) * P], m2[:, at:at + 96], cbd, start=True, stop=True)
                last.then_inc(full, 1)
            pe.wait_ge(s_aD, ab + A_HI)
            pe.wait_ge(s_bD, bb + B_HI)
            for n in range(N_HI):
                out, full = ring(n, A_HI, B_HI)
                for s in range(2):
                    last = mm(out[:, s * 256:(s + 1) * 256], ss[:, n * 256 + s * P:n * 256 + (s + 1) * P],
                              fhi[0:96, :], start=True, stop=True)
                last.then_inc(full, 1)
            pe.wait_ge(s_aD, ab + A_T3)
            pe.wait_ge(s_bD, bb + B_T3)
            for n in range(N_T3):
                out, full = ring(n, A_T3, B_T3)
                for m in range(4):
                    at = (n // 4) * 1536 + (4 * (n % 4) + m) * 96
                    last = nc.tensor.transpose(out[0:96, m * P:(m + 1) * P], ci[:, at:at + 96], ident)
                last.then_inc(full, 1)

        def tower(g):
            sg, ab, bb, wb = g * (STAGES * STEPS), g * A_GROUP, g * B_GROUP, g * (LAYERS * 96)
            stage("first", sg, None, ab, bb, g * 64, wb)
            with pe.Fori(0, LAYERS - 1) as l:
                stage("mid", sg + STEPS + l * STEPS, l, ab + A_FWD + l * A_FWD, bb + B_FWD + l * B_FWD, None,
                      wb + 96 + l * 96)
            stage("last", sg + 4 * STEPS, 3, ab + 4 * A_FWD, bb + 4 * B_FWD, None, None)

        tower(0)
        ffn.between(pe, ffn.pe_event, 0, BETWEEN_FIRST)
        with pe.Fori(1, GROUPS) as g:
            pe.wait_ge(ffn.s_between, g)
            tower(g)
            ffn.between(pe, ffn.pe_event, g, BETWEEN)
        ffn.tail(pe, ffn.pe_event)

    @block.scalar
    def _(act):
        A = nc.scalar.activation
        act.wait_ge(s_prep, 1)
        A(wconv[:, :], bank(0), ACT.Identity).then_inc(s_prepc, 1)

        def stage(kind, sg, l, ab, bb, dcb):
            def sq_step(i):
                act.wait_ge(s_y, sg + i + 1)
                if i >= 2:
                    act.wait_ge(s_ssq, sg + i - 1)
                A(sq[:, (i % 2) * BANK:(i % 2 + 1) * BANK], y_bank[i % 2], ACT.Square, scale=WIDTH ** -0.5)
                if i >= 8:
                    act.wait_ge(s_t1, sg + i - 7)
                A(yz[:, (i % 8) * BANK:(i % 8 + 1) * BANK], y_bank[i % 2], ACT.Identity).then_inc(s_sq, 1)

            def h_step(i):
                act.wait_ge(s_t1, sg + i + 1)
                fn = ACT.Gelu if kind == "mid" else ACT.Identity
                if i == 0:
                    act.wait_ge(s_ln, 16 * stage.index + 16)
                A(pixel_run(h, i // 8, i), t_bank[i % 2].rearrange("p (j x) -> p j x", x=P), fn,
                  scale=lnc[:, 0:1], bias=lnc[:, 1:2]).then_inc(s_h, 1)

            def w_step(i):
                at = a_wdft(i)
                act.wait_ge(s_aF, ab + at + 1)
                r, q = i % 8, i // 8
                dst = cw[:, (q % 2) * NKY * P:(q % 2 + 1) * NKY * P].rearrange(
                    "p (k u j f x) -> p u f j k x", k=NKY, u=4, j=4, f=2)[:, r // 2, r % 2]
                src = a_bank[at % 2][:, 0:384].rearrange("p (j z) -> p j z", z=96)[:, :, 0:48].rearrange(
                    "p j (k x) -> p j k x", x=4)
                A(dst, src, ACT.Identity).then_inc(s_aD, 1)

            def tc_step(q, k):
                at = a_tc(q, k)
                act.wait_ge(s_aF, ab + at + 1)
                s, e = q // 2, q % 2
                dst = dk[:, s * 8 * 384:(s + 1) * 8 * 384].rearrange(
                    "p (g e k c) -> p e g k c", g=4, e=2, k=NKY)[:, e, :, 4 * k:4 * k + 4, :]
                src = a_bank[at % 2].rearrange("p (k g c) -> p g k c", k=4, g=4)
                A(dst, src, ACT.Identity).then_inc(s_aD, 1)

            if kind == "last":
                for i in range(STEPS + LAG_T2 + 1):
                    if i < STEPS:
                        sq_step(i)
                    if 0 <= i - LAG_T1 < STEPS:
                        h_step(i - LAG_T1)
                    n = i - LAG_T2
                    if 0 <= n < STEPS:
                        for k in range(4):
                            at = a_fc1(n, k)
                            act.wait_ge(s_aF, ab + at + 1)
                            A(z1[:, (n % 2) * 2048 + k * BANK:(n % 2) * 2048 + (k + 1) * BANK], a_bank[at % 2],
                              ACT.Gelu, bias=fc1_b).then_inc(s_aD, 1)
                    n -= 1
                    if 0 <= n < STEPS:
                        for k in range(2):
                            at = a_fc2(n, k)
                            act.wait_ge(s_aF, ab + at + 1)
                            if n >= 2:
                                act.wait_ge(s_bF, bb + n - 1)
                            A(z2[:, (n % 2) * 1024 + k * BANK:(n % 2) * 1024 + (k + 1) * BANK], a_bank[at % 2],
                              ACT.Gelu, bias=fc2_b).then_inc(s_aD, 1)
                return
            for i in range(STEPS + LAG_W):
                if i < STEPS:
                    sq_step(i)
                if 0 <= i - LAG_T1 < STEPS:
                    h_step(i - LAG_T1)
                if 0 <= i - LAG_W < STEPS:
                    w_step(i - LAG_W)
                    if (i - LAG_W) % 8 == 7:
                        for k in range(3):
                            tc_step((i - LAG_W) // 8, k)

            def even(total, a0):
                for n in range(0, total, 2):
                    act.wait_ge(s_aF, ab + a0 + n // 2 + 1)
                    yield n, a_bank[(a0 + n // 2) % 2]

            for n, src in even(N_F3, A_F3):
                A(f3_dst(xs, n), f3_src(src), ACT.Identity).then_inc(s_aD, 1)
            for n, src in even(N_MIX, A_MIX):
                done = A(mix_dst(m2, n), mix_src(src), ACT.Identity)
                if n == 0:
                    done.then_inc(s_dc, 1)
                    act.wait_ge(s_dcc, 16 * dcb + 16)
                    A(dcs[:, :], dcc[:, 2:3], ACT.Identity, scale=float(PX)).then_inc(s_dc, 1)
                    act.wait_ge(s_dc, 2 * dcb + 2)
                    done = A(m2[0:32, 0:768].rearrange("p (m z) -> p m z", z=48)[:, :, 0], src[0:32, 0:16],
                             ACT.Identity, bias=dcs[:, :])
                done.then_inc(s_aD, 1)
            for n, src in even(N_TS, A_TS):
                A(ts_dst(ss, n), ts_src(src), ACT.Identity).then_inc(s_aD, 1)
            for n, src in even(N_HI, A_HI):
                A(hi_dst(ci, n), hi_src(src), ACT.Identity).then_inc(s_aD, 1)
            for n, src in even(N_T3, A_T3):
                A(gi[0:96, n * BANK:(n + 1) * BANK], src[0:96, :], ACT.Identity).then_inc(s_aD, 1)

        def tower(g):
            sg, ab, bb = g * (STAGES * STEPS), g * A_GROUP, g * B_GROUP
            stage.index = g * STAGES
            stage("first", sg, 0, ab, bb, g * LAYERS)
            with act.Fori(1, LAYERS) as l:
                stage.index = g * STAGES + l
                stage("mid", sg + l * STEPS, l, ab + l * A_FWD, bb + l * B_FWD, g * LAYERS + l)
            stage.index = g * STAGES + LAYERS
            stage("last", sg + 4 * STEPS, 4, ab + 4 * A_FWD, bb + 4 * B_FWD, None)

        tower(0)
        ffn.between(act, ffn.act_event, 0, BETWEEN_FIRST)
        with act.Fori(1, GROUPS) as g:
            act.wait_ge(ffn.s_between, g)
            tower(g)
            ffn.between(act, ffn.act_event, g, BETWEEN)
        ffn.tail(act, ffn.act_event)

    @block.vector
    def _(dve):
        V = nc.vector
        V.memset(xg[:, :], 0.0).then_inc(s_init, 1)
        V.memset(wx[:, :], 0.0).then_inc(s_init, 1)
        dve.wait_ge(s_init, 2)
        dve.wait_ge(s_prep, 1)
        V.tensor_copy(wx[0:13, :], bank(1)[0:13, 0:P]).then_inc(s_prepc, 1)

        nrb = reads = None

        def read_piece(n):
            if reads is not None:
                g, l = reads
                ffn.unit_half(dve, g - 1, EARLY * HEADS + STAGE_UNITS * l, n // 2, n % 2)

        def stage(kind, sg, ab, bb):
            def sum_step(i):
                dve.wait_ge(s_sq, sg + i + 1)
                b = (i // 4) % 2
                if i % 4 == 0 and i >= 8:
                    dve.wait_ge(s_z, sg + i - 4)
                V.tensor_reduce(ssq[:, b * 64 + (i % 4) * 16:b * 64 + (i % 4 + 1) * 16],
                                sq[:, (i % 2) * BANK:(i % 2 + 1) * BANK].rearrange("p (a c) -> p a c", c=WIDTH),
                                AX.X, ALU.add).then_inc(s_ssq, 1)

            def rsqrt_batch(n):
                nb = sg // 4 * NR if isinstance(sg, int) else None
                base = nrb(sg, n)
                half = slice((n % 2) * 64, (n % 2 + 1) * 64)
                v, y, t = ssq[:, half], rs[:, half], rt[:, half]
                k = 0

                def link(ins):
                    nonlocal k
                    k += 1
                    ins.then_inc(s_nr, 1)
                    dve.wait_ge(s_nr, base + k)

                dve.wait_ge(s_ssq, sg + 4 * n + 4)
                link(V.tensor_scalar(v, v, EPS, None, ALU.add))
                link(V.tensor_scalar(t.bitcast(I32), v.bitcast(I32), 1, None, ALU.logical_shift_right))
                link(V.tensor_scalar(y.bitcast(I32), t.bitcast(I32), -1.0, MAGIC, ALU.mult, ALU.add))
                for _ in range(3):
                    link(V.scalar_tensor_tensor(t, y, -0.5, y, ALU.mult, ALU.mult))
                    link(V.tensor_tensor(t, t, v, ALU.mult))
                    link(V.scalar_tensor_tensor(y, t, 1.5, y, ALU.add, ALU.mult))
                link(V.tensor_copy(t, y))
                assert k == NR

            def z_step(i):
                z = yz[:, (i % 8) * BANK:(i % 8 + 1) * BANK].rearrange("p (a c) -> p a c", c=WIDTH)
                b = (i // 4) % 2
                r = rs[:, b * 64 + (i % 4) * 16:b * 64 + (i % 4 + 1) * 16].unsqueeze(2).broadcast_to([P, 16, WIDTH])
                V.tensor_tensor(z, z, r, ALU.mult).then_inc(s_z, 1)

            def t2_step(i):
                dve.wait_ge(s_bF, bb + i + 1)
                if i >= 2:
                    dve.wait_ge(s_aF, ab + a_wdft(i - 2) + 1)
                V.tensor_copy(pl[:, (i % 2) * BANK:(i % 2 + 1) * BANK], b_bank[i % 2]).then_inc(s_bD, 1)

            def fc3_step(i):
                dve.wait_ge(s_bF, bb + i + 1)
                if i >= 2:
                    dve.wait_ge(s_out[i % 2], outb + 64 * (i // 2))
                V.tensor_scalar(o3[:, (i % 2) * BANK:(i % 2 + 1) * BANK], b_bank[i % 2][0:64, :], fc3_b[0:64, :],
                                None, ALU.add).then_inc(s_bD, 1)

            lag3 = LAG_T2 + 2 if kind == "last" else LAG_T2
            outb = stage.outb
            for i in range(STEPS + lag3 + 1):
                if i < STEPS:
                    sum_step(i)
                if i < STEPS and i % 4 == 3:
                    rsqrt_batch(i // 4)
                if 0 <= i - 4 < STEPS:
                    z_step(i - 4)
                if 0 <= i - lag3 < STEPS:
                    (fc3_step if kind == "last" else t2_step)(i - lag3)
                if i % LOOP_EVERY[kind] == 1 and i // LOOP_EVERY[kind] < (
                        2 * STAGE_UNITS if kind == "last" else LOOP_PIECES):
                    read_piece(i // LOOP_EVERY[kind])
            if kind == "last":
                return

            def odd(total, b0):
                for n in range(1, total, 2):
                    dve.wait_ge(s_bF, bb + b0 + n // 2 + 1)
                    yield n, b_bank[(b0 + n // 2) % 2]
                    jobs = b0 + n // 2 - B_F3 + 1
                    if jobs % 5 == 0 and LOOP_PIECES + jobs // 5 <= 2 * STAGE_UNITS:
                        read_piece(LOOP_PIECES + jobs // 5 - 1)

            for n, src in odd(N_F3, B_F3):
                V.tensor_copy(f3_dst(xs, n), f3_src(src)).then_inc(s_bD, 1)
            for n, src in odd(N_MIX, B_MIX):
                V.tensor_copy(mix_dst(m2, n), mix_src(src)).then_inc(s_bD, 1)
            for n, src in odd(N_TS, B_TS):
                V.tensor_copy(ts_dst(ss, n), ts_src(src)).then_inc(s_bD, 1)
            for n, src in odd(N_HI, B_HI):
                V.tensor_copy(hi_dst(ci, n), hi_src(src)).then_inc(s_bD, 1)
            for n, src in odd(N_T3, B_T3):
                V.tensor_copy(gi[0:96, n * BANK:(n + 1) * BANK], src[0:96, :]).then_inc(s_bD, 1)

        def tower(g, units):
            nonlocal nrb, reads
            sg, ab, bb = g * (STAGES * STEPS), g * A_GROUP, g * B_GROUP
            nr0 = g * (STAGES * 8 * NR)
            stage.outb = g * (STEPS // 2 * 64)
            nrb = lambda sg_, n: nr0 + n * NR
            reads = (g, 0) if units else None
            stage("first", sg, ab, bb)
            with dve.Fori(1, LAYERS) as l:
                nrb = lambda sg_, n: nr0 + l * (8 * NR) + n * NR
                reads = (g, l) if units else None
                stage("mid", sg + l * STEPS, ab + l * A_FWD, bb + l * B_FWD)
            nrb = lambda sg_, n: nr0 + (4 * 8 + n) * NR
            reads = (g, LAYERS) if units else None
            stage("last", sg + 4 * STEPS, ab + 4 * A_FWD, bb + 4 * B_FWD)

        for k in range(GB):
            V.memset(ffn.count[:, k:k + 1], 0.0).then_inc(ffn.s_ws, 1)
        tower(0, False)
        ffn.between(dve, ffn.dve_event, 0, BETWEEN_FIRST)
        with dve.Fori(1, GROUPS) as g:
            tower(g, True)
            ffn.between(dve, ffn.dve_event, g, BETWEEN)
        ffn.tail(dve, ffn.dve_event)


def f3_dst(xs, n):
    kyg, i4 = n // 4, n % 4
    return xs[:, kyg * 1536:(kyg + 1) * 1536].rearrange("p (z m) -> p m z", m=16)[:, 4 * i4:4 * i4 + 4, :]


def f3_src(bank):
    return bank[:, 0:384].rearrange("p (m z) -> p m z", m=4)


def mix_dst(m2, n):
    kyg, k4 = n // 6, n % 6
    return m2[:, kyg * 768:(kyg + 1) * 768].rearrange("p (m k r) -> p k r m", m=16, k=24)[:, 4 * k4:4 * k4 + 4]


def mix_src(bank):
    return bank[:, 0:384].rearrange("p (k z) -> p k z", k=4)[:, :, 0:32].rearrange("p k (r m) -> p k r m", r=2)


def ts_dst(ss, n):
    kyg, s = n // 2, n % 2
    return ss[:, kyg * 1024:(kyg + 1) * 1024].rearrange("p (k s g c) -> p s g k c", k=4, s=2, g=4)[:, s]


def ts_src(bank):
    return bank[0:96, :].rearrange("p (g k c) -> p g k c", g=4, k=4)


def hi_dst(ci, n):
    return ci[:, :].rearrange("p (q h k r) -> p k q h r", q=4, h=64, k=12)[:, n]


def hi_src(bank):
    return bank.rearrange("p (q h r) -> p q h r", q=4, r=2)


def dft_constants():
    kx = np.array(list(range(M1)) + list(range(H - M1, H)))
    w = np.arange(W)
    ident = np.eye(P)
    fw = np.zeros((2, W, NKY, 2, 2))
    fh = np.zeros((H, 2, NKX, 4))
    fhi = np.zeros((2, NKX, 2, 2, H, 2))
    fwi = np.zeros((4, NKY, 2, 2, 2, W))
    for k in range(NKY):
        a = 2 * np.pi * k * w / W
        for r in range(2):
            fw[r, :, k, r, 0] = np.cos(a)
            fw[r, :, k, r, 1] = -np.sin(a)
            for f in range(2):
                fwi[2 * f + r, k, 0, f, r] = np.cos(a) * (2 if k else 1) / W
                fwi[2 * f + r, k, 1, f, r] = -np.sin(a) * (2 if k else 0) / W
    a = 2 * np.pi * np.outer(np.arange(H), kx) / H
    for v, (re, im) in enumerate(((np.cos(a), np.sin(a)), (-np.sin(a), np.cos(a)),
                                  (np.sin(a), -np.cos(a)), (np.cos(a), np.sin(a)))):
        fh[:, 0, :, v] = re
        fh[:, 1, :, v] = im
    for e in range(2):
        fhi[e, :, 0, e, :, 0] = np.cos(a.T) / H
        fhi[e, :, 0, e, :, 1] = np.sin(a.T) / H
        fhi[e, :, 1, e, :, 0] = -np.sin(a.T) / H
        fhi[e, :, 1, e, :, 1] = np.cos(a.T) / H
    cbd = np.kron(np.eye(4), np.eye(WIDTH) - 1.0 / WIDTH)
    pad = lambda m, n: np.concatenate([m, np.zeros((P - m.shape[0], n))], 0) if m.shape[0] < P else m
    fwp = np.zeros((P, 96))
    fwp[:, 0:48] = fw.reshape(P, 48)
    return [ident, fwp, fh.reshape(P, 96), pad(fhi.reshape(96, 256), 256), pad(fwi.reshape(96, 256), 256), cbd]


def lay_out(a):
    f = np.float32
    get = lambda n: np.asarray(a["L0_tok_" + n])
    x = np.asarray(a["x"]).reshape(4, 2, 4, 2, PX, CH).transpose(0, 1, 3, 2, 5, 4).reshape(4 * 4 * 12, PX)
    w = np.stack([np.concatenate([get("w1" + r), get("w2" + r)], 3) for r in "ri"])
    w = w.reshape(2, LAYERS, WIDTH, WIDTH, NKX, 3, 4).transpose(1, 6, 2, 5, 4, 0, 3)
    modes = np.zeros((LAYERS, CHUNKS, 4, WIDTH, CH_MODES, 2, 4, WIDTH), f)
    w = w.reshape(LAYERS, 4, WIDTH, CHUNKS, CH_MODES, 2, WIDTH)
    for k in range(4):
        modes[:, :, k, :, :, :, k, :] = w[:, k].transpose(0, 2, 1, 3, 4, 5)
    consts = [m.astype(f) for m in dft_constants()]
    conv = np.zeros((4, WIDTH, LAYERS, 4, WIDTH), f)
    fc0 = np.zeros((4, WIDTH, 16), f)
    fc1 = np.zeros((4, WIDTH, 4, P), f)
    fc3 = np.zeros((2, 64, 32), f)
    for g in range(4):
        conv[g, :, :, g, :] = get("conv_w").transpose(1, 0, 2)
        fc0[g, :, 3 * g:3 * g + 3] = get("fc0_w").T
        fc0[g, :, 12] = get("fc0_b")
        fc1[g, :, g, :] = get("fc1_w")
    for g in range(2):
        fc3[g, :, g] = get("fc3_w")[:, 0]
    cols = np.zeros((P, 4), f)
    cols[:, 0] = get("fc1_b")
    cols[:, 1] = np.tile(get("fc2_b"), 2)
    cols[:, 2] = get("fc3_b")[0]
    ln = np.zeros((STAGES, P, 4), f)
    ln[0, :, 0], ln[0, :, 1] = np.tile(get("ln0_g"), 4), np.tile(get("ln0_b"), 4)
    ln[1:, :, 0], ln[1:, :, 1] = np.tile(get("ln_g"), (1, 4)), np.tile(get("ln_b"), (1, 4))
    ln[0:LAYERS, 0:32, 2] = get("conv_b")
    consts += [fc1.reshape(P, 512), get("fc2_w"), fc3.reshape(P, 32), cols]
    return {"setup": np.concatenate([conv.reshape(P, 512), fc0.reshape(P, 16)], 1), "x": np.ascontiguousarray(x), "ones": np.ones((1, PX), f),
            "ln": ln.reshape(STAGES * P, 4), "modes": modes.reshape(LAYERS * CHUNKS * P, 1024), "consts": np.concatenate(consts, 1)}


TILE = P
TILES = 8
HEADS, NK, TOPK, DIM = 8, 64, 16, 64
ROWS_AB = [(0, 1, 16), (1, 1, 8), (2, 1, 5), (3, 1, 4), (4, 1, 3), (5, 3, 2), (8, 8, 1)]
CELLS = sum(r * n for _, r, n in ROWS_AB)
NEG = -3.0e38
PRE = ["hT", "qkv", "att", "ctx", "res1", "h1T", "qpk", "sim0", "sim1"]
POST = ["h1Tq", "qT", "kT", "s0", "pT0", "o0", "s1", "pT1", "o1", "oT", "res2"]
SELECT = ["best", "pick0", "pick1", "pick2", "pick3", "norm"]
JOBS = PRE + POST
EARLY = 3
GB = 2
V_PRE, V_POST = 47, 16


def merge(lists):
    slots, order = max(len(x) for x in lists), []
    for k in range(slots):
        for x in lists:
            order += x[k * len(x) // slots:(k + 1) * len(x) // slots]
    return order


def between_order(first):
    order, units = [], 0
    for s in range(TILES + 2):
        post = [(n, s) for n in POST] if s < TILES and not first else []
        pre = [(n, s - 1) for n in PRE] if 1 <= s <= TILES else []
        select = [(n, s - 2) for n in SELECT] if s >= 2 else []
        until = max(0, s - 2) * EARLY * HEADS // (TILES - 1)
        order += merge([post, pre, select, [("unit%d" % (n % HEADS), n // HEADS) for n in range(units, until)]])
        units = until
    return order


def tail_order():
    order = merge([[(n, s) for s in range(EARLY) for n in POST], [("unit%d" % u, EARLY) for u in range(HEADS)]])
    for s in range(EARLY, TILES):
        units = [("unit%d" % u, s + 1) for u in range(HEADS)] if s + 1 < TILES else []
        order += merge([[(n, s) for n in POST], units])
    return order


BETWEEN_FIRST, BETWEEN = between_order(True), between_order(False)


class Ffn:

    def __init__(self, nc, c, d, hs, kvd, out, keep, mem, bank):
        self.nc = nc
        self.d, self.hs, self.kvd, self.out, self.bank = d, hs, kvd, out, bank
        sem = lambda n: c.enter_context(nc.semaphore(n))
        cst = mem(d["consts2"].shape[1])
        self.cst = cst
        off = 0

        def take(n):
            nonlocal off
            off += n
            return cst[:, off - n:off]

        self.ident, self.wqpk, self.wq, self.keys, self.wo = take(128), take(512), take(512), take(1024), take(256)
        self.aw = take(256)
        self.mask1, self.mask2, self.hoff, self.iota = take(128), take(128), take(128), take(CELLS)
        self.gb = keep(GB * 2048)
        self.iu, self.wt = keep(TILES * 128), keep(TILES * 128)
        self.h1 = keep(TILES * 64)
        self.kvs = keep(4 * 128)
        self.count = keep(GB)
        self.hin = mem(2 * 64)
        self.hT, self.qk, self.v1, self.att, self.ctx = mem(128), mem(256), mem(64), mem(128), mem(128)
        self.h1T, self.h1Tq = mem(128), mem(128)
        self.st = mem(16)
        self.qpk, self.sims = mem(512), mem(512)
        self.top, self.ti = mem(256), mem(256)
        self.jf = mem(256)
        self.cand, self.cidx = mem(HEADS * CELLS), mem(HEADS * CELLS)
        self.cv, self.cp, self.cpf = mem(128), mem(128), mem(128)
        self.oh = mem(2 * TOPK * CELLS)
        self.fi = mem(128)
        self.wsum = mem(16)
        self.kv = mem(2 * 1024)
        self.kT, self.qT, self.s, self.pT, self.o, self.oT = mem(512), mem(512), mem(512), mem(512), mem(512), mem(512)
        self.nmax, self.psum_, self.prec = mem(8), mem(8), mem(8)
        self.res = mem(2 * 64)
        self.s_const = sem("s_const2")
        self.s_hin = [sem("s_hin0"), sem("s_hin1")]
        self.s_fF, self.s_fD = sem("s_fF"), sem("s_fD")
        self.s_v = sem("s_v")
        self.s_top = sem("s_top")
        self.s_sub, self.s_exp = sem("s_sub"), sem("s_exp")
        self.s_idx = sem("s_idx")
        self.s_gath = [sem("s_gath%d" % i) for i in range(4)]
        self.s_ws = sem("s_ws")
        self.s_res1 = sem("s_res1")
        self.s_mx, self.s_p = sem("s_mx"), sem("s_p")
        self.s_u = sem("s_u")
        self.s_kvs = [sem("s_kvs%d" % i) for i in range(4)]
        self.s_kvl = [sem("s_kvl0"), sem("s_kvl1")]
        self.s_between = sem("s_between")
        self.s_fin = sem("s_fin")
        self.s_store = [sem("s_store0"), sem("s_store1")]
        self.vn = 0

    def sp_rows(self, sp, g, j):
        if j >= 2:
            sp.wait_ge(self.s_res1, g * TILES + j - 1)
        sp.dma_start(self.hin[:, (j % 2) * 64:(j % 2 + 1) * 64],
                     self.hs[bass.ds((g * TILES + j) * TILE, TILE), :]).then_inc(self.s_hin[j % 2], 16)

    def sp_kv(self, sp, g, j):
        if j >= 2:
            sp.wait_ge(self.s_fin, g * TILES + j - 1)
            self.settled(sp)
        for i in range(4):
            sp.wait_ge(self.s_kvs[i], g * (TILES * 32) + 32 * (j + 1))
            self.settled(sp)
        sp.dma_start(self.kv[:, (j % 2) * 1024:(j % 2 + 1) * 1024],
                     self.kvd[bass.ds((g * TILES + j) * TILE, TILE), :]).then_inc(self.s_kvl[j % 2], 16)

    def sp_store(self, sp, g, j):
        sp.wait_ge(self.s_fin, g * TILES + j + 1)
        sp.dma_start(self.out[bass.ds((g * TILES + j) * TILE, TILE), :],
                     self.res[:, (j % 2) * 64:(j % 2 + 1) * 64]).then_inc(self.s_store[j % 2], 16)

    def sp_between(self, sp, g, order):
        sp.dma_start(self.cst, self.d["consts2"]).then_inc(self.s_const, 16)
        post = order is BETWEEN
        if post:
            self.sp_kv(sp, g - 1, 0)
        for j in range(TILES):
            self.sp_rows(sp, g, j)
            if post:
                if j + 1 < TILES:
                    self.sp_kv(sp, g - 1, j + 1)
                self.sp_store(sp, g - 1, j)
        if post:
            for k in range(2):
                sp.wait_ge(self.s_store[k], g * (TILES // 2 * 16))
                self.settled(sp)

    def sp_tail(self, sp):
        self.sp_kv(sp, GROUPS - 1, 0)
        for j in range(TILES):
            if j + 1 < TILES:
                self.sp_kv(sp, GROUPS - 1, j + 1)
            self.sp_store(sp, GROUPS - 1, j)
        for k in range(2):
            sp.wait_ge(self.s_store[k], GROUPS * (TILES // 2 * 16))

    def between(self, engine, event, g, order):
        engine.wait_ge(self.s_const, g * 16 + 16)
        self.settled(engine)
        jobs = [e for e in order if e[0] in JOBS]
        self.at = {e: n for n, e in enumerate(jobs)}
        if order is BETWEEN_FIRST:
            self.fbase = self.vbase = 0
        else:
            self.fbase = TILES * len(PRE) + (g - 1) * len(jobs)
            self.vbase = TILES * V_PRE + (g - 1) * (TILES * (V_PRE + V_POST))
        self.vn = 0
        for kind, j in order:
            event(engine, g - 1 if kind in POST else g, kind, j)
        if event == self.dve_event:
            assert self.vn == TILES * (V_PRE + (V_POST if order is BETWEEN else 0)), self.vn
            engine.wait_ge(self.s_fD, self.fbase + len(jobs))
            self.nc.vector.memset(self.count[:, 0:1], 0.0).then_inc(self.s_between, 1)

    def tail(self, engine, event):
        order = tail_order()
        jobs = [e for e in order if e[0] in JOBS]
        self.at = {e: n for n, e in enumerate(jobs)}
        self.fbase = TILES * len(PRE) + (GROUPS - 1) * TILES * len(JOBS)
        self.vbase, self.vn = TILES * V_PRE + (GROUPS - 1) * (TILES * (V_PRE + V_POST)), 0
        for kind, j in order:
            event(engine, GROUPS - 1, kind, j)

    def settled(self, engine):
        engine.nop(nofuse=True)

    def pool_store(self, pool, g, n):
        dst = self.kvd[bass.ds((g * TILES + n // HEADS) * TILE, TILE), :]
        dst = dst.rearrange("p (w h x) -> p w h x", w=2, h=HEADS)[:, :, n % HEADS]
        src = self.kvs[:, (n % 4) * 128:(n % 4 + 1) * 128].rearrange("p (w x) -> p w x", w=2)
        pool.dma_start(dst, src).then_inc(self.s_kvs[n % 4], 16)

    def pool_group(self, pool, g):
        for n in range(TILES * HEADS):
            if n % HEADS == 0:
                pool.wait_ge(self.s_idx, g * TILES + n // HEADS + 1)
            pool.wait_ge(self.s_ws, g * (TILES * HEADS) + n + 1)
            self.settled(pool)
            if n >= GB:
                self.pool_store(pool, g, n - GB)
            for k in range(TOPK):
                at = (n % GB) * 2048 + k * 128
                col = n * TOPK + k
                self.nc.gpsimd.indirect_dma_start(
                    out=self.gb[:, at:at + 128], out_offset=None, in_=self.d["kv"],
                    in_offset=bass.IndirectOffsetOnAxis(ap=self.iu[:, col:col + 1].bitcast(U32), axis=0),
                ).then_inc(self.s_gath[n % 4], 16)
        for n in range(TILES * HEADS - GB, TILES * HEADS):
            pool.wait_ge(self.s_ws, g * (TILES * HEADS) + n + 1 + GB)
            self.settled(pool)
            self.pool_store(pool, g, n)

    def pe_event(self, pe, g, kind, j):
        if kind not in JOBS:
            return
        nc, mm = self.nc, self.nc.tensor.matmul
        f = self.fbase + self.at[(kind, j)]
        b = self.bank
        t = g * TILES + j
        if not isinstance(f, int) or f > 0:
            pe.wait_ge(self.s_fD, f)
        if kind in ("qkv", "h1Tq"):
            self.settled(pe)
        h1T = self.h1T
        kk = self.kv[:, (j % 2) * 1024:(j % 2) * 1024 + 512]
        vv = self.kv[:, (j % 2) * 1024 + 512:(j % 2 + 1) * 1024]
        if kind == "hT":
            pe.wait_ge(self.s_hin[j % 2], g * (TILES // 2 * 16) + 16 * (j // 2 + 1))
            self.settled(pe)
            last = nc.tensor.transpose(b[0:64, 0:P], self.hin[:, (j % 2) * 64:(j % 2 + 1) * 64], self.ident)
        elif kind == "qkv":
            mm(b[0:64, 0:P], self.aw[0:64, 0:64], self.hT[0:64, :], start=True, stop=True)
            mm(b[0:64, P:2 * P], self.aw[0:64, 64:128], self.hT[0:64, :], start=True, stop=True)
            last = mm(b[:, 2 * P:2 * P + 64], self.hT[0:64, :], self.aw[0:64, 128:192], start=True, stop=True)
        elif kind == "att":
            last = mm(b[:, 0:P], self.qk[0:64, P:2 * P], self.qk[0:64, 0:P], start=True, stop=True)
        elif kind == "ctx":
            last = mm(b[0:64, 0:P], self.v1, self.att, start=True, stop=True)
        elif kind == "res1":
            last = mm(b[:, 0:64], self.ctx[0:64, :], self.aw[0:64, 192:256], start=True, stop=True)
        elif kind == "h1T":
            pe.wait_ge(self.s_res1, t + 1)
            self.settled(pe)
            last = nc.tensor.transpose(b[0:64, 0:P], self.h1[:, j * 64:(j + 1) * 64], self.ident)
        elif kind == "h1Tq":
            last = nc.tensor.transpose(b[0:64, 0:P], self.h1[:, j * 64:(j + 1) * 64], self.ident)
        elif kind == "qpk":
            for m in range(4):
                last = mm(b[:, m * P:(m + 1) * P], self.wqpk[0:64, m * P:(m + 1) * P], h1T[0:64, :],
                          start=True, stop=True)
        elif kind in ("sim0", "sim1"):
            p = int(kind[3])
            for m in range(2):
                last = mm(b[:, m * 256:(m + 1) * 256], self.qpk[:, (2 * p + m) * P:(2 * p + m + 1) * P],
                          self.keys[:, (2 * p + m) * 256:(2 * p + m + 1) * 256], start=True, stop=True)
        elif kind == "qT":
            for m in range(4):
                last = mm(b[:, m * P:(m + 1) * P], self.wq[0:64, m * P:(m + 1) * P], self.h1Tq[0:64, :],
                          start=True, stop=True)
        elif kind == "kT":
            pe.wait_ge(self.s_kvl[j % 2], g * (TILES // 2 * 16) + 16 * (j // 2 + 1))
            self.settled(pe)
            for m in range(4):
                last = nc.tensor.transpose(b[:, m * P:(m + 1) * P], kk[:, m * P:(m + 1) * P], self.ident)
        elif kind in ("s0", "s1"):
            hf = int(kind[1])
            for m in range(4):
                rows, col = slice(64 * hf, 64 * hf + 64), slice(m * P, (m + 1) * P)
                last = mm(b[:, m * P:(m + 1) * P], self.qT[rows, col], self.kT[rows, col], start=True, stop=True)
        elif kind in ("pT0", "pT1"):
            pe.wait_ge(self.s_p, 2 * t + int(kind[2]) + 1)
            for m in range(4):
                last = nc.tensor.transpose(b[:, m * P:(m + 1) * P], self.s[:, m * P:(m + 1) * P], self.ident)
        elif kind in ("o0", "o1"):
            for m in range(4):
                hd = 2 * m + int(kind[1])
                last = mm(b[:, m * 64:(m + 1) * 64], self.pT[:, m * P:(m + 1) * P], vv[:, hd * 64:(hd + 1) * 64],
                          start=True, stop=True)
        elif kind == "oT":
            for m in range(4):
                last = nc.tensor.transpose(b[:, m * P:(m + 1) * P], self.o[:, m * P:(m + 1) * P], self.ident)
        elif kind == "res2":
            for m in range(4):
                last = mm(b[:, 0:64], self.oT[:, m * P:(m + 1) * P], self.wo[:, m * 64:(m + 1) * 64],
                          start=(m == 0), stop=(m == 3))
        last.then_inc(self.s_fF, 1)

    def act_event(self, act, g, kind, j):
        A = self.nc.scalar.activation
        f = None
        if kind in JOBS:
            f = self.fbase + self.at[(kind, j)]
        t = g * TILES + j
        b = self.bank
        h1T = self.h1T
        plain = {"hT": (self.hT[0:64, :], b[0:64, 0:P]), "ctx": (self.ctx[0:64, :], b[0:64, 0:P]),
                 "h1T": (h1T[0:64, :], b[0:64, 0:P]), "h1Tq": (self.h1Tq[0:64, :], b[0:64, 0:P]), "qpk": (self.qpk, b), "kT": (self.kT, b),
                 "sim0": (self.sims, b), "sim1": (self.sims, b), "pT0": (self.pT, b), "pT1": (self.pT, b),
                 "oT": (self.oT, b)}
        if kind in plain:
            act.wait_ge(self.s_fF, f + 1)
            if kind in ("sim0", "sim1"):
                top = 2 * t + int(kind[3])
                if not isinstance(top, int) or top > 0:
                    act.wait_ge(self.s_top, top)
            A(plain[kind][0], plain[kind][1], ACT.Identity).then_inc(self.s_fD, 1)
        elif kind == "qkv":
            act.wait_ge(self.s_fF, f + 1)
            A(self.qk[0:64, :], b[0:64, 0:2 * P], ACT.Identity)
            A(self.v1, b[:, 2 * P:2 * P + 64], ACT.Identity).then_inc(self.s_fD, 1)
        elif kind == "qT":
            act.wait_ge(self.s_fF, f + 1)
            A(self.qT, b, ACT.Identity, scale=DIM ** -0.5).then_inc(self.s_fD, 1)
        elif kind == "best":
            act.wait_ge(self.s_sub, t + 1)
            w = self.wt[:, j * 128:(j + 1) * 128]
            A(w, w, ACT.Exp).then_inc(self.s_exp, 1)
        elif kind in ("s0", "s1"):
            act.wait_ge(self.s_mx, 2 * t + int(kind[1]) + 1)
            for m in range(4):
                hd = 4 * int(kind[1]) + m
                last = A(self.s[:, m * P:(m + 1) * P], self.s[:, m * P:(m + 1) * P], ACT.Exp,
                         bias=self.nmax[:, hd:hd + 1], accum_out=self.psum_[:, hd:hd + 1])
            last.then_inc(self.s_p, 1)

    def link(self, dve, ins):
        self.vn += 1
        ins.then_inc(self.s_v, 1)
        dve.wait_ge(self.s_v, self.vbase + self.vn)

    def unit_half(self, dve, g, first, n, half):
        V = self.nc.vector
        rows = self.gb[:, (n % GB) * 2048:(n % GB + 1) * 2048].rearrange("p (k x) -> p k x", k=TOPK)
        unit = g * (TILES * HEADS) + first + n
        if half == 0:
            dve.wait_ge(self.s_gath[n % 4], (g * (TILES * HEADS) + first) * 64 + 256 * (n // 4 + 1))
            w = self.wt[:, (first + n) * TOPK:(first + n + 1) * TOPK] if isinstance(first, int) else \
                self.wt[:, bass.ds((first + n) * TOPK, TOPK)]
            V.tensor_tensor(rows, rows, w.unsqueeze(2).broadcast_to([P, TOPK, 128]), ALU.mult).then_inc(self.s_u, 1)
        else:
            free = (g * (TILES * HEADS) + first) * 4 + 16 * (n // 4)
            if not isinstance(free, int) or free > 0:
                dve.wait_ge(self.s_kvs[n % 4], free)
            dve.wait_ge(self.s_u, unit + 1)
            V.tensor_reduce(self.kvs[:, (n % 4) * 128:(n % 4 + 1) * 128], rows.rearrange("p k x -> p x k"), AX.X,
                            ALU.add).then_inc(self.s_ws, 1)

    def layer_norm(self, dve, src, dst, done):
        V, st = self.nc.vector, self.st
        mv, v, y, t = st[:, 6:8], st[:, 7:8], st[:, 8:9], st[:, 9:10]
        L = lambda ins: self.link(dve, ins)
        L(V.bn_stats(st[:, 0:6], src))
        self.settled(dve)
        L(V.bn_aggr(mv, st[:, 0:6]))
        L(V.tensor_scalar(v, v, EPS, None, ALU.add))
        L(V.tensor_scalar(t.bitcast(I32), v.bitcast(I32), 1, None, ALU.logical_shift_right))
        L(V.tensor_scalar(y.bitcast(I32), t.bitcast(I32), -1.0, MAGIC, ALU.mult, ALU.add))
        for _ in range(3):
            L(V.scalar_tensor_tensor(t, y, -0.5, y, ALU.mult, ALU.mult))
            L(V.tensor_tensor(t, t, v, ALU.mult))
            L(V.scalar_tensor_tensor(y, t, 1.5, y, ALU.add, ALU.mult))
        V.tensor_scalar(dst, src, mv[:, 0:1], y, ALU.subtract, ALU.mult).then_inc(done, 1)

    def top16(self, dve, src, vals, idx, seg):
        V = self.nc.vector
        for r in range(2):
            sl = lambda x, h: x[:, h * 16 + 8 * r:h * 16 + 8 * r + 8]
            for h in range(HEADS):
                last = V.max(sl(vals, h), src[:, h * seg:(h + 1) * seg])
            self.link(dve, last)
            self.settled(dve)
            for h in range(HEADS):
                last = V.max_index(sl(idx, h).bitcast(U32), sl(vals, h), src[:, h * seg:(h + 1) * seg])
            self.link(dve, last)
            self.settled(dve)
            if r == 0:
                for h in range(HEADS):
                    x = src[:, h * seg:(h + 1) * seg]
                    last = V.match_replace(x, sl(vals, h), x, NEG)
                self.link(dve, last)
                self.settled(dve)

    def dve_event(self, dve, g, kind, j):
        nc, V = self.nc, self.nc.vector
        f = self.fbase + self.at[(kind, j)] if kind in JOBS else None
        t = g * TILES + j
        b = self.bank
        link = lambda ins: self.link(dve, ins)
        h1 = self.h1[:, j * 64:(j + 1) * 64]
        w = self.wt[:, j * 128:(j + 1) * 128]
        if kind == "att":
            dve.wait_ge(self.s_fF, f + 1)
            V.scalar_tensor_tensor(self.att, b[:, 0:P], 0.0, self.mask1, ALU.max, ALU.mult).then_inc(self.s_fD, 1)
        elif kind == "res1":
            dve.wait_ge(self.s_fF, f + 1)
            ins = V.tensor_tensor(h1, self.hin[:, (j % 2) * 64:(j % 2 + 1) * 64], b[:, 0:64], ALU.add)
            ins.then_inc(self.s_fD, 1)
            dve.wait_ge(self.s_fD, f + 1)
            self.layer_norm(dve, h1, h1, self.s_res1)
        elif kind in ("sim0", "sim1"):
            dve.wait_ge(self.s_fD, f + 1)
            p = int(kind[3])
            self.settled(dve)
            self.top16(dve, self.sims, self.top[:, 128 * p:128 * (p + 1)], self.ti[:, 128 * p:128 * (p + 1)], NK)
            V.tensor_copy(self.jf[:, 128 * p:128 * (p + 1)],
                          self.ti[:, 128 * p:128 * (p + 1)].bitcast(U32)).then_inc(self.s_top, 1)
        elif kind == "best":
            dve.wait_ge(self.s_top, 2 * t + 2)
            j1 = self.jf[:, 128:256]
            link(V.scalar_tensor_tensor(j1, j1, float(NK), self.hoff, ALU.mult, ALU.add))
            for x, y in ((self.top, self.cand), (self.jf, self.cidx)):
                c3 = y[:, :].rearrange("p (h n) -> p h n", h=HEADS)
                x0 = x[:, 0:128].rearrange("p (h n) -> p h n", h=HEADS)
                x1 = x[:, 128:256].rearrange("p (h n) -> p h n", h=HEADS)
                at = 0
                for a, rows, n in ROWS_AB:
                    o = c3[:, :, at:at + rows * n]
                    if rows == 1:
                        i0, i1 = x0[:, :, a:a + 1].broadcast_to([P, HEADS, n]), x1[:, :, 0:n]
                    elif n == 1:
                        i0, i1 = x0[:, :, a:a + rows], x1[:, :, 0:1].broadcast_to([P, HEADS, rows])
                    else:
                        o = o.rearrange("p h (r n) -> p h r n", r=rows)
                        i0 = x0[:, :, a:a + rows].unsqueeze(3).broadcast_to([P, HEADS, rows, n])
                        i1 = x1[:, :, 0:n].unsqueeze(2).broadcast_to([P, HEADS, rows, n])
                    last = V.tensor_tensor(o, i0, i1, ALU.add)
                    at += rows * n
            link(last)
            self.settled(dve)
            self.top16(dve, self.cand, self.cv, self.cp, CELLS)
            v3 = self.cv[:, :].rearrange("p (h n) -> p h n", h=HEADS)
            w3 = w.rearrange("p (h n) -> p h n", h=HEADS)
            V.tensor_tensor(w3, v3, v3[:, :, 0:1].broadcast_to([P, HEADS, TOPK]), ALU.subtract).then_inc(self.s_sub, 1)
            link(V.tensor_copy(self.cpf, self.cp.bitcast(U32)))
        elif kind.startswith("pick"):
            h2 = 2 * int(kind[4])
            sh = [P, 2, TOPK, CELLS]
            oh = self.oh[:, :].rearrange("p (h k n) -> p h k n", h=2, k=TOPK)
            ohf = self.oh[:, :].rearrange("p (x n) -> p x n", n=CELLS)
            link(V.tensor_tensor(ohf, self.cpf[:, h2 * TOPK:(h2 + 2) * TOPK].unsqueeze(2).broadcast_to(
                [P, 2 * TOPK, CELLS]), self.iota.unsqueeze(1).broadcast_to([P, 2 * TOPK, CELLS]), ALU.is_equal))
            ci = self.cidx[:, h2 * CELLS:(h2 + 2) * CELLS].rearrange("p (h n) -> p h n", h=2)
            link(V.tensor_tensor(oh, oh, ci.unsqueeze(2).broadcast_to(sh), ALU.mult))
            link(V.tensor_reduce(self.fi[:, h2 * TOPK:(h2 + 2) * TOPK], ohf, AX.X, ALU.add))
            if h2 == HEADS - 2:
                V.tensor_copy(self.iu[:, j * 128:(j + 1) * 128].bitcast(U32), self.fi).then_inc(self.s_idx, 1)
        elif kind == "norm":
            w3 = w.rearrange("p (h n) -> p h n", h=HEADS)
            dve.wait_ge(self.s_exp, t + 1)
            link(V.tensor_reduce(self.wsum[:, 0:8], w3, AX.X, ALU.add))
            link(V.reciprocal(self.wsum[:, 8:16], self.wsum[:, 0:8]))
            link(V.tensor_tensor(w3, w3, self.wsum[:, 8:16].unsqueeze(2).broadcast_to([P, HEADS, TOPK]), ALU.mult))
        elif kind.startswith("unit"):
            n = HEADS * j + int(kind[4:])
            for half in range(2):
                self.unit_half(dve, g, n // 4 * 4, n % 4, half)
        elif kind in ("s0", "s1"):
            dve.wait_ge(self.s_fF, f + 1)
            hf = int(kind[1])
            s3 = self.s[:, :].rearrange("p (h n) -> p h n", h=4)
            V.tensor_tensor(s3, b.rearrange("p (h n) -> p h n", h=4),
                            self.mask2.unsqueeze(1).broadcast_to([P, 4, P]), ALU.add).then_inc(self.s_fD, 1)
            dve.wait_ge(self.s_fD, f + 1)
            V.tensor_reduce(self.nmax[:, 4 * hf:4 * hf + 4], s3, AX.X, ALU.max, negate=True).then_inc(self.s_mx, 1)
        elif kind in ("o0", "o1"):
            hf = int(kind[1])
            dve.wait_ge(self.s_fF, f + 1)
            link(V.reciprocal(self.prec[:, 4 * hf:4 * hf + 4], self.psum_[:, 4 * hf:4 * hf + 4]))
            V.tensor_tensor(self.o[:, :].rearrange("p (m f x) -> p f m x", m=4, f=2)[:, hf],
                            b[:, 0:256].rearrange("p (h x) -> p h x", h=4),
                            self.prec[:, 4 * hf:4 * hf + 4].unsqueeze(2).broadcast_to([P, 4, 64]),
                            ALU.mult).then_inc(self.s_fD, 1)
        elif kind == "res2":
            dve.wait_ge(self.s_fF, f + 1)
            res = self.res[:, (j % 2) * 64:(j % 2 + 1) * 64]
            if j >= 2:
                dve.wait_ge(self.s_store[j % 2], g * (TILES // 2 * 16) + 16 * (j // 2))
            V.tensor_tensor(res, h1, b[:, 0:64], ALU.add).then_inc(self.s_fD, 1)
            dve.wait_ge(self.s_fD, f + 1)
            self.layer_norm(dve, res, res, self.s_fin)


def lay_out_ffn(a):
    f = np.float32
    aw = np.concatenate([np.asarray(a["L0_attn_W" + n]).T for n in "qkvo"], 1)
    pad = lambda m: np.concatenate([m, np.zeros((P - m.shape[0], m.shape[1]), f)], 0)
    keys = np.zeros((2, 2, 4, 32, 4, NK), f)
    pk = np.asarray(a["L0_ffn_pk_keys"]).transpose(0, 2, 3, 1).reshape(2, 2, 4, 32, NK)
    for m in range(4):
        keys[:, :, m, :, m, :] = pk[:, :, m]
    keys = keys.reshape(4, P, 256).transpose(1, 0, 2).reshape(P, 1024)
    wo = np.asarray(a["L0_ffn_Wo"]).reshape(4, P, DIM).transpose(1, 0, 2).reshape(P, 256)
    i = np.arange(P)
    same = (i[:, None] // 64) == (i[None, :] // 64)
    mask1 = np.where(same & (i[:, None] <= i[None, :]), 1.0 / np.maximum(i % 64, 1)[None, :], 0.0).astype(f)
    mask2 = np.where(same & (i[None, :] <= i[:, None]), 0.0, NEG).astype(f)
    hoff = np.broadcast_to(np.repeat(np.arange(HEADS) * NK * NK, TOPK).astype(f), (P, 128))
    iota = np.broadcast_to(np.arange(CELLS).astype(f), (P, CELLS))
    return {"consts2": np.concatenate([np.eye(P, dtype=f), pad(np.asarray(a["L0_ffn_Wq_pk"])),
                                       pad(np.asarray(a["L0_ffn_Wq"])), keys, wo, pad(aw), mask1, mask2, hoff, iota], 1),
            "kv": np.concatenate([np.asarray(a["L0_ffn_keys_table"]), np.asarray(a["L0_ffn_values_table"])], 1)}



def kernel(**inputs):
    import concourse.bacc as bacc
    from concourse.bass_utils import run_bass_kernel_spmd

    arrays = {**lay_out(inputs), **lay_out_ffn(inputs)}
    nc = bacc.Bacc("TRN2", target_bir_lowering=False, num_devices=1)
    arrays = {"in_" + n: np.ascontiguousarray(a) for n, a in arrays.items()}
    d = {n[3:]: nc.dram_tensor(n, a.shape, mybir.dt.from_np(a.dtype), kind="ExternalInput").ap()
         for n, a in arrays.items()}
    hs = nc.dram_tensor("tower", (B, PX), F32, kind="Internal").ap()
    out = nc.dram_tensor("out_0", (B * H, W), F32, kind="ExternalOutput").ap()
    kvd = nc.dram_tensor("token_kv", (B * H, 2 * HEADS * DIM), F32, kind="Internal").ap()
    with ExitStack() as c:
        build(nc, c, d, hs, kvd, out)
    r = run_bass_kernel_spmd(nc, [arrays], core_ids=[0])
    return r.results[0]["out_0"].reshape(B, H, W)
```
